# Optimizing a Trainium2 kernel written in Bass

```python
import numpy as np
import jax
import jax.numpy as jnp

def _softmax(x, axis=-1):
    return jax.nn.softmax(x, axis=axis)

def _gelu(x):
    return jax.nn.gelu(x, approximate=True)

def _silu(x):
    return jax.nn.silu(x)

def _sigmoid(x):
    return jax.nn.sigmoid(x)

def _layernorm(x, axis=-1, eps=1e-05):
    m = jnp.mean(x, axis=axis, keepdims=True)
    v = jnp.var(x, axis=axis, keepdims=True)
    return (x - m) / jnp.sqrt(v + eps)

def _scatter_add(tgt, idx, src, axis=0):
    return tgt.at[idx].add(src)

def _segment_sum(src, seg, n):
    return jax.ops.segment_sum(src, seg, n)
kernel_name = 'mk_seq_postln_d1_jaxref_r8_557d6e'

def setup_inputs(seed: int=0):
    np.random.seed(seed)
    _w = jnp.asarray

    def _L0_attn_setup():
        import math
        import jax, jax.numpy as jnp
        import numpy as np
        E = 128
        H = 16
        KVH = 8
        N_REP = H // KVH
        HD = E // H // 2
        DEPTH = 12
        LAMBDA_INIT = 0.8 - 0.6 * math.exp(-0.3 * DEPTH)
        EPS = 1e-06
        ROPE_BASE = 10000.0

        def rope_tables(T):
            inv_freq = 1.0 / ROPE_BASE ** (np.arange(0, HD, 2, dtype=np.float32) / HD)
            t = np.arange(T, dtype=np.float32)
            freqs = np.outer(t, inv_freq)
            return (jnp.asarray(np.cos(freqs)), jnp.asarray(np.sin(freqs)))

        def apply_rope(x, cos, sin):
            d = x.shape[-1] // 2
            c = cos[None, :, None, :]
            s = sin[None, :, None, :]
            x1, x2 = (x[..., :d], x[..., d:])
            return jnp.concatenate([x1 * c + x2 * s, -x1 * s + x2 * c], axis=-1)

        def causal_attn(q, k, v, scale):
            T = q.shape[1]
            mask = jnp.tril(jnp.ones((T, T), dtype=bool))
            s = jnp.einsum('bthd,bshd->bhts', q, k) * scale
            s = jnp.where(mask[None, None], s, jnp.finfo(s.dtype).min)
            p = jax.nn.softmax(s, axis=-1)
            return jnp.einsum('bhts,bshd->bthd', p, v)
        key = jax.random.key(seed)
        ks = jax.random.split(key, 10)
        s = 0.02
        return {'x': jax.random.normal(ks[0], (4, 128, E), jnp.float32), 'Wq': jax.random.normal(ks[1], (E, E), jnp.float32) * s, 'Wk': jax.random.normal(ks[2], (E, E // N_REP), jnp.float32) * s, 'Wv': jax.random.normal(ks[3], (E, E // N_REP), jnp.float32) * s, 'Wo': jax.random.normal(ks[4], (E, E), jnp.float32) * s, 'lambda_q1': jax.random.normal(ks[5], (HD,), jnp.float32) * 0.1, 'lambda_k1': jax.random.normal(ks[6], (HD,), jnp.float32) * 0.1, 'lambda_q2': jax.random.normal(ks[7], (HD,), jnp.float32) * 0.1, 'lambda_k2': jax.random.normal(ks[8], (HD,), jnp.float32) * 0.1, 'rms_w': jnp.ones((2 * HD,), jnp.float32)}
    _L0_attn_in = _L0_attn_setup()

    def _L0_ffn_setup():
        import jax, jax.numpy as jnp
        import numpy as np
        B, S, DIM, FFN, E = (4, 256, 128, 512, 8)
        key = jax.random.key(seed)
        k0, k1, k2, k3 = jax.random.split(key, 4)
        scale = 0.02
        return {'hidden_states': jax.random.normal(k0, (B, S, DIM), jnp.float32), 'router_w': jax.random.normal(k1, (DIM, E), jnp.float32) * scale, 'router_b': jnp.zeros((E,), jnp.float32), 'w1': jax.random.normal(k2, (E, DIM, 2 * FFN), jnp.float32) * scale, 'w2': jax.random.normal(k3, (E, FFN, DIM), jnp.float32) * scale}
    _L0_ffn_in = _L0_ffn_setup()
    _d = {'L0_attn_x': _L0_attn_in['x'], 'L0_attn_Wq': _L0_attn_in['Wq'], 'L0_attn_Wk': _L0_attn_in['Wk'], 'L0_attn_Wv': _L0_attn_in['Wv'], 'L0_attn_Wo': _L0_attn_in['Wo'], 'L0_attn_lambda_q1': _L0_attn_in['lambda_q1'], 'L0_attn_lambda_k1': _L0_attn_in['lambda_k1'], 'L0_attn_lambda_q2': _L0_attn_in['lambda_q2'], 'L0_attn_lambda_k2': _L0_attn_in['lambda_k2'], 'L0_attn_rms_w': _L0_attn_in['rms_w'], 'L0_ffn_router_w': _L0_ffn_in['router_w'], 'L0_ffn_router_b': _L0_ffn_in['router_b'], 'L0_ffn_w1': _L0_ffn_in['w1'], 'L0_ffn_w2': _L0_ffn_in['w2']}
    _x0 = _d['L0_attn_x']
    _d['L0_attn_x'] = jax.random.normal(jax.random.fold_in(jax.random.key(seed), 1), (8, 512, 128), dtype=_x0.dtype)
    del _x0
    return _d

def reference(L0_attn_x, L0_attn_Wq, L0_attn_Wk, L0_attn_Wv, L0_attn_Wo, L0_attn_lambda_q1, L0_attn_lambda_k1, L0_attn_lambda_q2, L0_attn_lambda_k2, L0_attn_rms_w, L0_ffn_router_w, L0_ffn_router_b, L0_ffn_w1, L0_ffn_w2):

    def _L0_attn_ref(x, Wq, Wk, Wv, Wo, lambda_q1, lambda_k1, lambda_q2, lambda_k2, rms_w):
        import math
        import jax, jax.numpy as jnp
        import numpy as np
        E = 128
        H = 16
        KVH = 8
        N_REP = H // KVH
        HD = E // H // 2
        DEPTH = 12
        LAMBDA_INIT = 0.8 - 0.6 * math.exp(-0.3 * DEPTH)
        EPS = 1e-06
        ROPE_BASE = 10000.0

        def rope_tables(T):
            inv_freq = 1.0 / ROPE_BASE ** (np.arange(0, HD, 2, dtype=np.float32) / HD)
            t = np.arange(T, dtype=np.float32)
            freqs = np.outer(t, inv_freq)
            return (jnp.asarray(np.cos(freqs)), jnp.asarray(np.sin(freqs)))

        def apply_rope(x, cos, sin):
            d = x.shape[-1] // 2
            c = cos[None, :, None, :]
            s = sin[None, :, None, :]
            x1, x2 = (x[..., :d], x[..., d:])
            return jnp.concatenate([x1 * c + x2 * s, -x1 * s + x2 * c], axis=-1)

        def causal_attn(q, k, v, scale):
            T = q.shape[1]
            mask = jnp.tril(jnp.ones((T, T), dtype=bool))
            s = jnp.einsum('bthd,bshd->bhts', q, k) * scale
            s = jnp.where(mask[None, None], s, jnp.finfo(s.dtype).min)
            p = jax.nn.softmax(s, axis=-1)
            return jnp.einsum('bhts,bshd->bthd', p, v)
        B, T, _ = x.shape
        q = (x @ Wq).reshape(B, T, 2 * H, HD)
        k = (x @ Wk).reshape(B, T, 2 * KVH, HD)
        v = (x @ Wv).reshape(B, T, KVH, 2, HD)
        cos, sin = rope_tables(T)
        q = apply_rope(q, cos, sin)
        k = apply_rope(k, cos, sin)
        q = q.reshape(B, T, H, 2, HD)
        k = k.reshape(B, T, KVH, 2, HD)
        q1, q2 = (q[:, :, :, 0], q[:, :, :, 1])
        k1, k2 = (k[:, :, :, 0], k[:, :, :, 1])
        vcat = v.reshape(B, T, KVH, 2 * HD)
        k1 = jnp.repeat(k1, N_REP, axis=2)
        k2 = jnp.repeat(k2, N_REP, axis=2)
        vcat = jnp.repeat(vcat, N_REP, axis=2)
        scale = HD ** (-0.5)
        attn1 = causal_attn(q1, k1, vcat, scale)
        attn2 = causal_attn(q2, k2, vcat, scale)
        lambda_1 = jnp.exp(jnp.sum(lambda_q1 * lambda_k1))
        lambda_2 = jnp.exp(jnp.sum(lambda_q2 * lambda_k2))
        lambda_full = lambda_1 - lambda_2 + LAMBDA_INIT
        attn = attn1 - lambda_full * attn2
        rms = jnp.sqrt(jnp.mean(attn * attn, axis=-1, keepdims=True) + EPS)
        attn = attn / rms * rms_w
        attn = attn * (1.0 - LAMBDA_INIT)
        attn = attn.reshape(B, T, H * 2 * HD)
        return attn @ Wo

    def _L0_ffn_ref(hidden_states, router_w, router_b, w1, w2):
        import jax, jax.numpy as jnp
        import numpy as np
        B, S, DIM, FFN, E = (4, 256, 128, 512, 8)
        b, s, d = hidden_states.shape
        x = hidden_states.reshape(-1, d)
        logits = x @ router_w + router_b
        route = jax.nn.softmax(logits, axis=1)
        max_prob = jnp.max(route, axis=1, keepdims=True)
        max_ind = jnp.argmax(route, axis=1)
        out = jnp.zeros_like(x)
        num_experts = w1.shape[0]
        for e in range(num_experts):
            h = x @ w1[e]
            a, g = jnp.split(h, 2, axis=1)
            y = jax.nn.silu(a) * g @ w2[e]
            out = jnp.where((max_ind == e)[:, None], y, out)
        out = out * max_prob
        return out.reshape(b, s, d)
    x = L0_attn_x
    x = _layernorm(x + _L0_attn_ref(x, L0_attn_Wq, L0_attn_Wk, L0_attn_Wv, L0_attn_Wo, L0_attn_lambda_q1, L0_attn_lambda_k1, L0_attn_lambda_q2, L0_attn_lambda_k2, L0_attn_rms_w), axis=-1)
    x = _layernorm(x + _L0_ffn_ref(x, L0_ffn_router_w, L0_ffn_router_b, L0_ffn_w1, L0_ffn_w2), axis=-1)
    return x

_drawn_inputs = setup_inputs


def setup_inputs(seed=0):
    import zlib

    import numpy as np

    out = dict(_drawn_inputs(seed))
    spreads = {'L0_attn_rms_w': (1.0, 0.6), 'L0_ffn_router_b': (0.0, 0.8)}
    factors = {'L0_attn_Wq': 3.682,
     'L0_attn_Wk': 3.663,
     'L0_attn_lambda_q1': 8.0,
     'L0_attn_lambda_k1': 8.0,
     'L0_attn_lambda_q2': 8.0,
     'L0_attn_lambda_k2': 8.0,
     'L0_ffn_router_w': 8.0,
     'L0_ffn_w1': 8.0,
     'L0_ffn_w2': 8.0}
    for name, (base, spread) in spreads.items():
        noise = np.random.default_rng([zlib.crc32(name.encode()), seed]).standard_normal(out[name].shape)
        drawn = base * np.exp(spread * noise) if base else spread * noise
        out[name] = jnp.asarray(drawn.astype(out[name].dtype))
    for name, factor in factors.items():
        out[name] = (out[name] * factor).astype(out[name].dtype)
    return out
```

```python
import math
from contextlib import ExitStack

import numpy as np

import concourse.bass as bass
from concourse import mybir

F32 = mybir.dt.float32
BF16 = mybir.dt.bfloat16
U32 = mybir.dt.uint32
ALU = mybir.AluOpType
ACT = mybir.ActivationFunctionType
AX = mybir.AxisListType

B, T, E = 8, 512, 128
P = 128
H, KVH = 16, 8
HD = E // H // 2
NI = T // P
NX = 8
FFN = 512
NF = FFN // P
LAMBDA_INIT = 0.8 - 0.6 * math.exp(-0.3 * 12)
RMS_EPS, LN_EPS = 1e-6, 1e-5
MASKED = -1e30

Q_PART = [0, 0, 0, 1, 1, 2]
K_PART = [0, 1, 2, 0, 1, 0]
TERMS = len(Q_PART)
ROWS = TERMS * HD
MROWS = 3
VW = 2 * HD + 1

SUPER = KVH // 2
NS = B * SUPER
UNITS = ([("A", 0, c) for c in range(4)] + [("B", 0, c) for c in range(4)] + [("C", 0, c) for c in range(4)]
         + [("A", 1, c) for c in range(4)] + [("B", 1, c) for c in range(4)])
NU = len(UNITS)
GROUPS = [("A", 0, 0, 3), ("B", 0, 4, 7), ("C", 0, 8, 11), ("A", 1, 12, 15), ("C", 1, 8, 11), ("B", 1, 16, 19)]
NG = len(GROUPS)
LAST_GROUP = [0] * 4 + [1] * 4 + [4] * 4 + [3] * 4 + [5] * 4
PV_AT = {7: 0, 11: 1, 15: 2, 19: 3}
PV_TAIL_AT = {1: 4, 3: 5}

SLOT = 256
NSLOT = B * T // SLOT + NX - 1
NTILE = B * T // P

MISC = []
for _p in range(SUPER):
    MISC += [(_p, 1, "sel0"), (_p, 4, "turn_max"), (_p, 9, "sel1")]
MISC += [(0, 12, "q"), (0, 15, "q_swap"), (1, 12, "k"), (1, 15, "k_swap"), (3, 12, "v"),
         (2, 18, "turn_attn"), (3, 6, "wo"), (3, 15, "turn_x1"), (3, 18, "router")]
MISC.sort(key=lambda m: m[:2])
PREP = ["q", "q_swap", "k", "k_swap", "v"]
POST = ["turn_attn", "wo", "turn_x1", "router"]


def back(u):
    return u - 3 if u >= 3 else (-2, -1, -3)[u]


def on(b, p, lag):
    return not isinstance(b, int) or 0 <= SUPER * b + p - lag < NS


def used(b, p, name):
    if not isinstance(b, int):
        return True
    if name in PREP:
        return b + 1 < B
    if name in POST:
        return b >= 1
    return on(b, p, 1 if name == "turn_max" else 3)


def uses_before(b, p, name):
    n = len(PREP)
    whole = b if isinstance(b, int) else 1
    for i in range(whole):
        n += sum(used(i, m[0], m[2]) for m in MISC)
    if not isinstance(b, int):
        n = n + (b - 1) * len(MISC)
    for m in MISC:
        if (m[0], m[2]) == (p, name):
            return n
        n = n + (1 if used(b, m[0], m[2]) else 0)
    raise KeyError(name)


TOTAL_MISC = len(PREP) + sum(used(i, m[0], m[2]) for i in range(B + 1) for m in MISC)


def misc_at(b, p, u):
    return [m[2] for m in MISC if m[:2] == (p, u) and used(b, p, m[2])]


def build(nc, xT, x, wq, wqs, wk, wks, wv, wo, lam, rms, router_w, router_b, w12, c_rope, c_ident, c_mask,
          c_sel, c_tri, c_iota, c_one, out):
    with ExitStack() as ctx:
        def sb(name, shape, dt=F32):
            return ctx.enter_context(nc.sbuf_tensor(name, shape, dt))

        def bank(name, width=512):
            return ctx.enter_context(nc.psum_tensor(name, [P, width], F32))

        def sem(name):
            return ctx.enter_context(nc.semaphore(name))

        qk_parts = nc.dram_tensor("qk_parts", (B, 2, TERMS, 4, HD, KVH, T), BF16).ap()
        max_rows = nc.dram_tensor("max_rows", (NS, 3, 4, 2 * NI, P), BF16).ap()
        x_sorted = nc.dram_tensor("x_sorted", (NSLOT * SLOT, E), F32).ap()
        y_sorted = nc.dram_tensor("y_sorted", (NSLOT * SLOT, E), F32).ap()

        rope = sb("rope", [P, 4, T])
        ident = sb("ident", [P, P])
        ident_b = sb("ident_b", [P, P], BF16)
        mask_b = sb("mask_b", [P, P], BF16)
        sel = sb("sel", [P, 4 * VW])
        tri = sb("tri", [P, 2, P])
        iota = sb("iota", [P, 16 + NSLOT + NX + 1])
        wq_s = sb("wq_s", [P, 4, P])
        wv_s = sb("wv_s", [P, KVH * 2 * HD])
        wo_s = sb("wo_s", [P, P])
        wo_n = sb("wo_n", [P, P])
        lam_s = sb("lam_s", [P, 4, HD])
        lam_p = sb("lam_p", [P, 2, HD])
        lam_d = sb("lam_d", [P, 4])
        lam_n = sb("lam_n", [P, 1])
        rms_s = sb("rms_s", [P, 1])
        rms_c = sb("rms_c", [P, 1])
        rw_s = sb("rw_s", [P, NX])
        rb_s = sb("rb_s", [P, NX])
        half = sb("half", [P, NI])
        eps = sb("eps", [P, 1])

        xt_s = sb("xt_s", [P, T])
        rot1 = sb("rot1", [P, T])
        rot2 = sb("rot2", [P, T])
        rot = sb("rot", [P, T])
        rest = sb("rest", [P, T])
        parts = sb("parts", [P, 2, 3, T], BF16)
        v_new = sb("v_new", [P, NI, KVH, 2 * HD])
        v_aug = sb("v_aug", [P, NI, KVH, 32])
        qa = sb("qa", [P, KVH, T], BF16)
        ka = sb("ka", [P, 4, KVH, T], BF16)
        mr = sb("mr", [P, 2, 8, 7])
        mneg = sb("mneg", [P, 8, NI])
        mrest = sb("mrest", [P, 8, NI])
        msplit = sb("msplit", [P, 3, 8, NI], BF16)
        mturn = sb("mturn", [96, P], BF16)
        prob = sb("prob", [P, NU, T])
        ot = sb("ot", [P, 2, T])
        on_s = sb("on_s", [P, KVH, NI, 4, VW])
        rl = sb("rl", [P, KVH, NI, 4])
        at = sb("at", [P, KVH * NI * 4, 2 * HD])
        dif = sb("dif", [P, KVH, NI, 2, 2 * HD])
        sq = sb("sq", [P, KVH * NI * 2, 2 * HD])
        ss = sb("ss", [P, KVH * NI * 2])
        rln = sb("rln", [P, KVH * NI * 2])
        rg = sb("rg", [P, KVH * NI * 2])
        nv = sb("nv", [P, KVH * NI * 2])
        ny = sb("ny", [P, KVH * NI * 2])
        rinv = sb("rinv", [P, KVH * NI * 2])
        dn = sb("dn", [P, NI, KVH, 2, 2 * HD])
        dt_s = sb("dt_s", [P, T])
        xn = sb("xn", [P, NI, E])
        res = sb("res", [P, NI, E])
        bst = sb("bst", [P, NI, 6])
        bag = sb("bag", [P, NI, 2])
        vare = sb("vare", [P, NI])
        rstd = sb("rstd", [P, NI])
        x1 = sb("x1", [P, NI, E])
        x1t = sb("x1t", [P, T])
        x1_all = sb("x1_all", [P, NTILE, E])
        logit = sb("logit", [P, NTILE, NX])

        rt = {n: sb("rt_" + n, [P, NTILE, NX]) for n in ("d", "e", "t", "oh", "a", "b", "c", "z")}
        rmax = sb("rmax", [P, NTILE])
        rsum = sb("rsum", [P, NTILE])
        rmin = sb("rmin", [P, NTILE])
        maxp = sb("maxp", [P, NTILE])
        pos_f = sb("pos_f", [P, NTILE])
        pos_u = sb("pos_u", [P, NTILE], U32)
        cmp_n = sb("cmp_n", [P, NX, 16])
        nsl = sb("nsl", [P, 5, NX])
        cmp_s = sb("cmp_s", [P, NSLOT, NX - 1])
        es = sb("es", [P, NSLOT])
        es_r = sb("es_r", [P, NSLOT])
        es_u = sb("es_u", [P, NSLOT], U32)
        wbuf = sb("wbuf", [P, 2, 3 * FFN])
        xs = sb("xs", [P, 2, SLOT // P, E])
        xst = sb("xst", [P, 2, SLOT])
        sa = sb("sa", [P, NF, SLOT])
        u_s = sb("u_s", [P, 2, NF, SLOT])
        ys = sb("ys", [P, 2, SLOT // P, E])
        yg = prob[:, 0:NTILE * E // T, :].rearrange("p u (a d) -> p (u a) d", d=E)
        bst2 = sb("bst2", [P, NTILE, 6])
        bag2 = sb("bag2", [P, NTILE, 2])
        var2 = sb("var2", [P, NTILE])
        rstd2 = sb("rstd2", [P, NTILE])

        banks = [bank(f"bank{i}") for i in range(8)]
        nat_b, st_b, pv_b, misc = banks[0:3], banks[3:6], banks[6], banks[7]

        s_const = sem("s_const")
        s_xt = sem("s_xt")
        s_xn = sem("s_xn")
        s_half = sem("s_half")
        s_vzero = sem("s_vzero")
        s_lam = sem("s_lam")
        s_lexp = sem("s_lexp")
        s_won = sem("s_won")
        s_split = sem("s_split")
        s_written = [sem("s_written_q"), sem("s_written_k")]
        s_vnew = sem("s_vnew")
        s_vaug = sem("s_vaug")
        s_qk = [sem(f"s_qk{i}") for i in range(SUPER)]
        s_nat = sem("s_nat")
        s_max = sem("s_max")
        s_neg = sem("s_neg")
        s_mw = sem("s_mw")
        s_mrow = [sem(f"s_mrow{i}") for i in range(SUPER)]
        s_st = sem("s_st")
        s_exp = sem("s_exp")
        s_masked = sem("s_masked")
        s_pv = sem("s_pv")
        s_ot = sem("s_ot")
        s_misc = sem("s_misc")
        s_free = sem("s_free")
        s_rl = sem("s_rl")
        s_post = sem("s_post")
        s_ss = sem("s_ss")
        s_guess = sem("s_guess")
        s_newton = sem("s_newton")
        s_bn = sem("s_bn")
        s_x1 = sem("s_x1")
        s_x1st = sem("s_x1st")
        s_zero = sem("s_zero")
        s_clear = sem("s_clear")
        s_ones = sem("s_ones")
        s_xzero = sem("s_xzero")
        s_route = sem("s_route")
        s_rexp = sem("s_rexp")
        s_rank = sem("s_rank")
        s_pos = sem("s_pos")
        s_scat = sem("s_scat")
        s_wg = [sem("s_wg0"), sem("s_wg1")]
        s_xs = [sem("s_xs0"), sem("s_xs1")]
        s_xturn = sem("s_xturn")
        s_xst = sem("s_xst")
        s_h = sem("s_h")
        s_silu = sem("s_silu")
        s_u = sem("s_u")
        s_y = sem("s_y")
        s_ycopy = sem("s_ycopy")
        s_yst = [sem("s_yst0"), sem("s_yst1")]
        s_yg = [sem(f"s_yg{i}") for i in range(NTILE // 4)]
        s_res = sem("s_res")
        s_st2 = sem("s_st2")
        s_rs2 = sem("s_rs2")
        s_fin = sem("s_fin")
        s_out = sem("s_out")

        block = ctx.enter_context(nc.Block())

        def iterations(eng, body):
            body(0)
            with eng.Fori(1, B - 1) as b:
                body(b)
            body(B - 1)
            body(B)

        def wait(eng, s, n):
            if not isinstance(n, int) or n > 0:
                eng.wait_ge(s, n)

        consts = [(wq_s[:, 0, :], wq), (wq_s[:, 1, :], wqs), (wq_s[:, 2, :], wk), (wq_s[:, 3, :], wks),
                  (wv_s[:, :], wv), (rope[:, :, :], c_rope), (ident[:, :], c_ident), (wo_s[:, :], wo),
                  (sel[:, :], c_sel), (tri[:, :, :], c_tri), (iota[:, :], c_iota),
                  (ident_b[:, :], c_mask[:, 0:P]), (mask_b[:, :], c_mask[:, P:2 * P]),
                  (lam_s[:, :, :].rearrange("p a d -> p (a d)"), lam.partition_broadcast(P)),
                  (rw_s[:, :], router_w), (rms_s[:, :], rms), (rb_s[:, :], router_b.partition_broadcast(P))]
        ALL_CONST = 16 * len(consts)
        ones_of = [(ka[32 * c + ROWS:32 * c + ROWS + MROWS, c, :, :].rearrange("p k t -> p (k t)"), c_one[0:MROWS])
                   for c in range(4)]

        @block.sync
        def _(sp):
            def write_parts(bn, a):
                wait(sp, s_split, 10 * bn + 5 * a + 5)
                for term, part in enumerate((Q_PART, K_PART)[a]):
                    sp.dma_start(qk_parts[bn, a, term].rearrange("c d k t -> (c d k) t"),
                                 parts[:, a, part, :]).then_inc(s_written[a], 16)

            def load_slot(bn, q):
                if q == 0:
                    for a in range(2):
                        wait(sp, s_written[a], 16 * TERMS * (bn + 1))
                for c in range(4):
                    sp.dma_start(qa[32 * c + ROWS:32 * c + ROWS + MROWS, 2 * q:2 * q + 2, :]
                                 .rearrange("p k t -> p (k t)"), c_one[MROWS:, 0:2 * T]).then_inc(s_qk[q], 16)
                    for a, dst in enumerate((qa, ka[:, c])):
                        sp.dma_start(dst[32 * c:32 * c + ROWS, 2 * q:2 * q + 2, :].rearrange("p k t -> p (k t)"),
                                     qk_parts[bn, a, :, c, :, 2 * q:2 * q + 2, :].rearrange("r d k t -> r d (k t)"))\
                            .then_inc(s_qk[q], 16)

            sp.dma_start(xt_s[:, :], xT[:, 0:T]).then_inc(s_xt, 16)
            for dst, src in consts:
                sp.dma_start(dst, src).then_inc(s_const, 16)
            sp.dma_start(xn[:, :, :], x[0:T, :].rearrange("(i p) d -> p i d", p=P)).then_inc(s_xn, 16)
            sp.wait_ge(s_clear, 3)
            for dst, src in ones_of:
                sp.dma_start(dst, src).then_inc(s_ones, 16)
            for a in range(2):
                write_parts(0, a)
            for q in range(SUPER):
                load_slot(0, q)
            sp.wait_ge(s_free, len(PREP))
            sp.dma_start(xt_s[:, :], xT[:, T:2 * T]).then_inc(s_xt, 16)
            sp.wait_ge(s_zero, 1)
            zeros = x1_all[:, :, :].rearrange("p n d -> p (n d)")
            n0 = NTILE * P
            sp.dma_start(x_sorted[0:n0, :].rearrange("(p n) d -> p (n d)", p=P), zeros).then_inc(s_xzero, 16)
            sp.dma_start(x_sorted[n0:, :].rearrange("(p n) d -> p (n d)", p=P),
                         zeros[:, 0:(NSLOT * SLOT - n0) // P * E]).then_inc(s_xzero, 16)
            sp.wait_ge(s_xzero, 32)

            def body(b):
                for p in range(SUPER):
                    nxt = 4 * b + p + 1
                    if isinstance(b, int):
                        load = SUPER <= nxt < NS
                    else:
                        load = True
                    if load:
                        wait(sp, s_st, NU * (nxt - SUPER + 1))
                        load_slot(b + (p + 1) // SUPER, (p + 1) % SUPER)
                    if on(b, p, 1):
                        s = 4 * b + p - 1
                        q = (p + 3) % SUPER
                        wait(sp, s_free, uses_before(b, p, "turn_max") + 1)
                        sp.dma_start(max_rows[s].rearrange("k c i t -> (k c i) t"), mturn[:, :]).then_inc(s_mw, 16)
                        wait(sp, s_mw, 16 * (s + 1))
                        for c in range(4):
                            sp.dma_start(qa[32 * c + ROWS:32 * c + ROWS + MROWS, 2 * q:2 * q + 2, :]
                                         .rearrange("p k t -> p (k t)"),
                                         max_rows[s, :, c].rearrange("k i t -> k (i t)")).then_inc(s_mrow[q], 16)
                    if used(b, 0, "q") and p in (1, 2):
                        write_parts(b + 1, p - 1)
                    if p == 3 and (not isinstance(b, int) or b + 2 < B):
                        wait(sp, s_free, uses_before(b, 3, "v") + 1)
                        sp.dma_start(xt_s[:, :], xT[:, bass.ds((b + 2) * T, T)]).then_inc(s_xt, 16)
                    if p == 3 and used(b, 3, "wo"):
                        bb = b - 1
                        wait(sp, s_free, uses_before(b, 3, "wo") + 1)
                        if not isinstance(b, int) or b < B:
                            sp.dma_start(xn[:, :, :], x[bass.ds(b * T, T), :].rearrange("(i p) d -> p i d", p=P))\
                                .then_inc(s_xn, 16)
                        wait(sp, s_post, 10 * bb + 10)
                        sp.dma_start(x1_all[:, bass.ds(bb * NI, NI), :], x1[:, :, :]).then_inc(s_x1st, 16)

            body(0)
            with sp.Fori(1, B - 2) as b:
                body(b)
            body(B - 2)
            body(B - 1)
            body(B)
            sp.wait_ge(s_scat, 16 * NTILE)
            for j in range(NSLOT):
                if j >= 2:
                    sp.wait_ge(s_xturn, j - 1)
                sp.dma_start(xs[:, j % 2, :, :], x_sorted[j * SLOT:(j + 1) * SLOT, :]
                             .rearrange("(a p) d -> p a d", p=P)).then_inc(s_xs[j % 2], 16)
                if j >= 2:
                    sp.wait_ge(s_ycopy, j - 1)
                    sp.dma_start(y_sorted[(j - 2) * SLOT:(j - 1) * SLOT, :].rearrange("(a p) d -> p a d", p=P),
                                 ys[:, j % 2, :, :]).then_inc(s_yst[j % 2], 16)
            for j in range(NSLOT - 2, NSLOT):
                sp.wait_ge(s_ycopy, j + 1)
                sp.dma_start(y_sorted[j * SLOT:(j + 1) * SLOT, :].rearrange("(a p) d -> p a d", p=P),
                             ys[:, j % 2, :, :]).then_inc(s_yst[j % 2], 16)
            for g in range(NTILE // 4):
                sp.wait_ge(s_fin, 4 * (g + 1))
                sp.dma_start(out[g * T:(g + 1) * T, :].rearrange("(i p) d -> p i d", p=P),
                             yg[:, 4 * g:4 * g + 4, :]).then_inc(s_out, 16)
            sp.wait_ge(s_out, 16 * (NTILE // 4))

        @block.tensor
        def _(pe):
            def misc_wait(b, p, name):
                n = name if isinstance(name, int) else uses_before(b, p, name)
                wait(pe, s_free, n)

            def prep(name, bn, b=None, p=None):
                misc_wait(b, p, name if b is not None else PREP.index(name))
                if name == "q":
                    wait(pe, s_xt, 16 * (bn + 1))
                if name == "v":
                    for i in range(NI):
                        mm_ = pe.matmul(misc[:, 64 * i:64 * i + 64], xt_s[:, i * P:(i + 1) * P], wv_s[:, :],
                                        start=True, stop=True)
                else:
                    mm_ = pe.matmul(misc[:, :], wq_s[:, PREP.index(name), :], xt_s[:, :], start=True, stop=True)
                mm_.then_inc(s_misc, 1)

            def nat(b, p, u):
                kind, kk, c = UNITS[u]
                s = 4 * b + p
                bk = nat_b[u % 3]
                if u == 0:
                    wait(pe, s_qk[p], 16 * 12 * (b + 1))
                wait(pe, s_max, (NU + 1) * s + back(u) + (1 if u >= 3 else 0))

                def q(kv, i):
                    return qa[:, kv, i * P:(i + 1) * P]

                if kind == "A":
                    pe.matmul(bk[:, :], q(2 * p + kk, 3), ka[:, c, 2 * p + kk, :], start=True, stop=True)
                    m = pe.matmul(bk[:, 384:512], ident_b[:, :], mask_b[:, :], start=False, stop=True,
                                  skip_group_check=True)
                elif kind == "B":
                    pe.matmul(bk[:, 0:128], q(2 * p + kk, 0), ka[:, c, 2 * p + kk, 0:128], start=True, stop=True)
                    pe.matmul(bk[:, 128:512], q(2 * p + kk, 2), ka[:, c, 2 * p + kk, 0:384], start=False, stop=True,
                              skip_group_check=True)
                    pe.matmul(bk[:, 0:128], ident_b[:, :], mask_b[:, :], start=False, stop=True,
                              skip_group_check=True)
                    m = pe.matmul(bk[:, 384:512], ident_b[:, :], mask_b[:, :], start=False, stop=True,
                                  skip_group_check=True)
                else:
                    for h in range(2):
                        pe.matmul(bk[:, 256 * h:256 * h + 256], q(2 * p + h, 1), ka[:, c, 2 * p + h, 0:256],
                                  start=h == 0, stop=True, skip_group_check=h == 1)
                    for h in range(2):
                        m = pe.matmul(bk[:, 256 * h + 128:256 * h + 256], ident_b[:, :], mask_b[:, :], start=False,
                                      stop=True, skip_group_check=True)
                m.then_inc(s_nat, 1)

            def st(b, p, u):
                kind, kk, c = UNITS[u]
                s, q = 4 * b + p - 2, (p + 2) % SUPER
                bk = st_b[u % 3]
                if u == 0:
                    wait(pe, s_mrow[q], 16 * 4 * (b + (1 if p >= 2 else 0)))
                wait(pe, s_exp, NU * s + back(u) + 1)

                def k(kv, j):
                    return ka[:, c, kv, j * P:(j + 1) * P]

                if kind == "A":
                    m = pe.matmul(bk[:, :], k(2 * q + kk, 0), qa[:, 2 * q + kk, :], start=True, stop=True)
                elif kind == "B":
                    pe.matmul(bk[:, 0:384], k(2 * q + kk, 1), qa[:, 2 * q + kk, 128:512], start=True, stop=True)
                    m = pe.matmul(bk[:, 384:512], k(2 * q + kk, 3), qa[:, 2 * q + kk, 384:512], start=False,
                                  stop=True, skip_group_check=True)
                else:
                    for h in range(2):
                        m = pe.matmul(bk[:, 256 * h:256 * h + 256], k(2 * q + h, 2), qa[:, 2 * q + h, 256:512],
                                      start=h == 0, stop=True, skip_group_check=h == 1)
                m.then_inc(s_st, 1)

            def pv(s, g, first_of_batch, batch):
                kind, kk, u0, u1 = GROUPS[g]
                q = s[1]
                wait(pe, s_masked, NU * s[0] + u1 + 1)
                if g == 0:
                    wait(pe, s_ot, 2 * s[0])
                    if first_of_batch:
                        wait(pe, s_vaug, batch + 1)
                if g == 3:
                    wait(pe, s_ot, 2 * s[0] + 1)
                kv = 2 * q + kk
                spans = {"A": [(0, 0, 0)], "B": [(1, 128, 0), (3, 384, 384)], "C": [(2, 256, 256 * kk)]}[kind]
                for n, (j, t0, col) in enumerate(spans):
                    for c in range(4):
                        m = pe.matmul(pv_b[32 * c:32 * c + 32, t0:T], v_aug[:, j, kv, :],
                                      prob[:, u0 + c, col:col + T - t0], start=kind == "A",
                                      stop=True, skip_group_check=True)
                m.then_inc(s_pv, 1)

            def uses(b, p, u):
                for name in misc_at(b, p, u):
                    s = 4 * b + p - 3
                    if name in PREP:
                        prep(name, b + 1, b, p)
                        continue
                    misc_wait(b, p, name)
                    if name in ("sel0", "sel1"):
                        kk = int(name[3])
                        wait(pe, s_ot, 2 * s + kk + 1)
                        for i in range(NI):
                            m = pe.matmul(misc[:, 4 * VW * i:4 * VW * (i + 1)], ot[:, kk, i * P:(i + 1) * P],
                                          sel[:, :], start=True, stop=True)
                    elif name == "turn_max":
                        wait(pe, s_neg, 6 * (4 * b + p))
                        m = pe.transpose(misc[0:96, 0:P // 2].bitcast(BF16),
                                         msplit[:, :, :, :].rearrange("p k c i -> p (k c i)"), ident_b[:, :])
                    elif name == "turn_attn":
                        wait(pe, s_post, 10 * (b - 1) + 4)
                        for i in range(NI):
                            m = pe.transpose(misc[:, i * P:(i + 1) * P],
                                             dn[:, i, :, :, :].rearrange("p k r v -> p (k r v)"), ident[:, :])
                    elif name == "wo":
                        for i in range(NI):
                            m = pe.matmul(misc[:, i * P:(i + 1) * P], dt_s[:, i * P:(i + 1) * P], wo_n[:, :],
                                          start=True, stop=True)
                    elif name == "turn_x1":
                        wait(pe, s_post, 10 * (b - 1) + 10)
                        for i in range(NI):
                            m = pe.transpose(misc[:, i * P:(i + 1) * P], x1[:, i, :], ident[:, :])
                    elif name == "router":
                        for i in range(NI):
                            m = pe.matmul(misc[:, i * NX:(i + 1) * NX], x1t[:, i * P:(i + 1) * P], rw_s[:, :],
                                          start=True, stop=True)
                    m.then_inc(s_misc, 1)

            pe.wait_ge(s_const, ALL_CONST)
            for name in PREP:
                prep(name, 0)
            pe.wait_ge(s_won, 1)
            pe.wait_ge(s_ones, 64)

            def body(b):
                for p in range(SUPER):
                    for u in range(NU):
                        if on(b, p, 0):
                            nat(b, p, u)
                        if on(b, p, 2):
                            st(b, p, u)
                            if u in PV_AT:
                                pv((4 * b + p - 2, (p + 2) % SUPER), PV_AT[u], p == 2, b)
                        if on(b, p, 3) and u in PV_TAIL_AT:
                            pv((4 * b + p - 3, (p + 1) % SUPER), PV_TAIL_AT[u], False, None)
                        uses(b, p, u)

            iterations(pe, body)

            pe.wait_ge(s_route, 9)
            oh = rt["oh"][:, :, :].rearrange("p n e -> p (n e)")
            pe.matmul(banks[0][:, 0:NTILE * NX], tri[:, 0, :], oh, start=True, stop=True)
            pe.matmul(banks[1][:, 0:NTILE * NX], tri[:, 1, :], oh, start=True, stop=True).then_inc(s_rank, 1)

            def turn_x(k, j, par):
                wait(pe, s_xs[par], 16 * (k + 1))
                wait(pe, s_xst, j)
                for a in range(SLOT // P):
                    m = pe.transpose(banks[4][:, a * P:(a + 1) * P], xs[:, par, a, :], ident[:, :])
                m.then_inc(s_xturn, 1)

            def hidden(k, j, par):
                wait(pe, s_xst, j + 1)
                wait(pe, s_wg[par], 16 * (k + 1))
                for f in range(NF):
                    wait(pe, s_u, NF * (j - 1) + f + 1)
                    for h in range(2):
                        m = pe.matmul(banks[f][:, h * SLOT:(h + 1) * SLOT],
                                      wbuf[:, par, h * FFN + f * P:h * FFN + (f + 1) * P], xst[:, par, :],
                                      start=h == 0, stop=True, skip_group_check=h == 1)
                    m.then_inc(s_h, 1)

            def down(j, par):
                wait(pe, s_u, NF * (j + 1))
                wait(pe, s_ycopy, j - 1)
                for a in range(SLOT // P):
                    for f in range(NF):
                        m = pe.matmul(banks[5 + par][:, a * P:(a + 1) * P], u_s[:, par, f, a * P:(a + 1) * P],
                                      wbuf[:, par, 2 * FFN + f * P:2 * FFN + (f + 1) * P],
                                      start=f == 0, stop=f == NF - 1)
                m.then_inc(s_y, 1)

            pe.wait_ge(s_pos, 1)
            turn_x(0, 0, 0)
            hidden(0, 0, 0)
            turn_x(0, 1, 1)

            def pair(k):
                hidden(k, 2 * k + 1, 1)
                down(2 * k, 0)
                turn_x(k + 1, 2 * k + 2, 0)
                hidden(k + 1, 2 * k + 2, 0)
                down(2 * k + 1, 1)

            pair(0)
            turn_x(1, 3, 1)
            with pe.Fori(1, (NSLOT - 1) // 2 - 1) as k:
                pair(k)
                turn_x(k + 1, 2 * k + 3, 1)
            pair((NSLOT - 1) // 2 - 1)
            down(NSLOT - 1, 0)

        @block.scalar
        def _(act):
            act.wait_ge(s_lam, 2)
            nc.scalar.activation(lam_d[:, 2:4], lam_d[:, 0:2], ACT.Exp).then_inc(s_lexp, 1)

            def exp(b, p, u):
                s = 4 * b + p - 2
                wait(act, s_st, NU * s + u + 1)
                wait(act, s_pv, NG * (s - 1) + LAST_GROUP[u] + 1)
                nc.scalar.activation(prob[:, u, :], st_b[u % 3][:, :], ACT.Exp).then_inc(s_exp, 1)

            def take_v(n):
                act.wait_ge(s_misc, n + 1)
                nc.scalar.activation(v_new[:, :, :, :].rearrange("p i k v -> p (i k v)"), misc[:, 0:256],
                                     ACT.Copy).then_inc(s_free, 1)

            def take(b, p, u):
                for name in misc_at(b, p, u):
                    if name not in ("sel0", "sel1", "turn_max", "turn_attn", "turn_x1", "v"):
                        continue
                    n = uses_before(b, p, name)
                    if name == "v":
                        wait(act, s_vaug, b + 1)
                        take_v(n)
                        continue
                    if name == "turn_max":
                        wait(act, s_mw, 16 * (4 * b + p - 1))
                    if name in ("sel0", "sel1"):
                        s = 4 * b + p - 3
                        q = (p + 1) % SUPER
                        if q == 0 and name == "sel0":
                            wait(act, s_post, 10 * (b - 1) + 1)
                        wait(act, s_misc, n + 1)
                        nc.scalar.activation(on_s[:, 2 * q + int(name[3]), :, :, :]
                                             .rearrange("p i c v -> p (i c v)"), misc[:, 0:NI * 4 * VW],
                                             ACT.Copy).then_inc(s_free, 1)
                        continue
                    wait(act, s_misc, n + 1)
                    if name == "turn_max":
                        dst, src = mturn[:, :], misc[0:96, 0:P // 2].bitcast(BF16)
                    elif name == "turn_attn":
                        dst, src = dt_s[:, :], misc[:, :]
                    else:
                        dst, src = x1t[:, :], misc[:, :]
                    nc.scalar.activation(dst, src, ACT.Copy).then_inc(s_free, 1)

            def take_ot(s, kk):
                wait(act, s_pv, NG * s + (3 if kk == 0 else 6))
                nc.scalar.activation(ot[:, kk, :], pv_b[:, :], ACT.Copy).then_inc(s_ot, 1)

            take_v(4)

            def body(b):
                for p in range(SUPER):
                    for u in range(NU):
                        if on(b, p, 2):
                            exp(b, p, u)
                            if u == 17:
                                take_ot(4 * b + p - 2, 0)
                        if on(b, p, 3) and u == 5:
                            take_ot(4 * b + p - 3, 1)
                        if u:
                            take(b, p, u - 1)
                        if used(b, p, "wo") and (p, u) == (2, 14):
                            bb = b - 1
                            wait(act, s_ss, bb + 1)
                            wait(act, s_half, 2)
                            nc.scalar.activation(rln[:, :], ss[:, :], ACT.Ln, bias=eps[:, 0:1]).then_inc(s_guess, 1)
                            wait(act, s_guess, 2 * bb + 1)
                            nc.scalar.activation(rg[:, :], rln[:, :], ACT.Exp, scale=-0.5).then_inc(s_guess, 1)

            iterations(act, body)

            act.wait_ge(s_route, 2)
            nc.scalar.activation(rt["e"][:, :, :].rearrange("p n e -> p (n e)"),
                                 rt["d"][:, :, :].rearrange("p n e -> p (n e)"), ACT.Exp).then_inc(s_rexp, 1)

            def slot(j):
                for f in range(NF):
                    wait(act, s_h, NF * j + f + 1)
                    wait(act, s_u, NF * (j - 1) + f + 1)
                    nc.scalar.activation(sa[:, f, :], banks[f][:, 0:SLOT], ACT.Silu).then_inc(s_silu, 1)

            def take_y(j, par):
                wait(act, s_y, j + 1)
                nc.scalar.activation(ys[:, par, :, :].rearrange("p a d -> p (a d)"), banks[5 + par][:, 0:SLOT],
                                     ACT.Copy).then_inc(s_ycopy, 1)

            slot(0)
            for j in range(1, 3):
                slot(j)
                take_y(j - 1, (j - 1) % 2)
            with act.Fori(1, (NSLOT - 1) // 2) as k:
                for n in range(2):
                    slot(2 * k + 1 + n)
                    wait(act, s_yst[n], 16 * k)
                    take_y(2 * k + n, n)
            act.wait_ge(s_yst[0], 16 * ((NSLOT - 1) // 2))
            take_y(NSLOT - 1, 0)

        @block.gpsimd
        def _(pool):
            def pwait(s, n):
                wait(pool, s, n)
                if not isinstance(n, int):
                    pool.nop(nofuse=True)

            pool.memset(ka[:, 2:4].rearrange("p c k t -> p (c k t)").bitcast(F32), 0.0).then_inc(s_clear, 1)
            pool.memset(half[:, :], -0.5).then_inc(s_half, 1)
            pool.memset(eps[:, :], 2 * HD * RMS_EPS).then_inc(s_half, 1)
            pool.memset(v_aug[:, :, :, :].rearrange("p i k v -> p (i k v)"), 0.0).then_inc(s_vzero, 1)
            pool.wait_ge(s_vzero, 1)
            pool.memset(v_aug[:, :, :, 2 * HD:VW].rearrange("p i k v -> p (i k) v"), 1.0).then_inc(s_vzero, 1)

            def split(bn, a, n_free):
                n = 10 * bn + 5 * a
                pwait(s_free, n_free)
                pwait(s_split, n)
                nc.gpsimd.tensor_tensor(rot[:, :], rot1[:, :], rot2[:, :], ALU.add).then_inc(s_split, 1)
                pwait(s_written[a], 16 * TERMS * bn)
                pwait(s_split, n + 1)
                nc.gpsimd.tensor_copy(parts[:, a, 0, :], rot[:, :]).then_inc(s_split, 1)
                pwait(s_split, n + 2)
                nc.gpsimd.tensor_tensor(rest[:, :], rot[:, :], parts[:, a, 0, :], ALU.subtract).then_inc(s_split, 1)
                pwait(s_split, n + 3)
                nc.gpsimd.tensor_copy(parts[:, a, 1, :], rest[:, :]).then_inc(s_split, 1)
                pwait(s_split, n + 4)
                nc.gpsimd.tensor_tensor(parts[:, a, 2, :], rest[:, :], parts[:, a, 1, :], ALU.subtract)\
                    .then_inc(s_split, 1)

            def mask(b, p, u):
                kind = UNITS[u][0]
                s = 4 * b + p - 2
                pwait(s_exp, NU * s + u + 1)
                if kind == "A":
                    v, pattern = prob[:, u, 0:P], [[1, P]]
                elif kind == "B":
                    v = prob[:, u, :].rearrange("p (n t) -> p n t", t=P)[:, 0:4:3, :]
                    pattern = [[0, 2], [1, P]]
                else:
                    v = prob[:, u, :].rearrange("p (n t) -> p n t", t=P)[:, 0:4:2, :]
                    pattern = [[0, 2], [1, P]]
                nc.gpsimd.affine_select(out=v, in_=v, compare_op=ALU.is_ge, fill=0.0, base=0, pattern=pattern,
                                        channel_multiplier=-1).then_inc(s_masked, 1)

            def negate(b, p):
                s = 4 * b + p - 1
                par = (p + 1) % 2
                n = 6 * s
                src = mr[:, par]
                pwait(s_max, (NU + 1) * (s + 1))
                pwait(s_neg, n)
                nc.gpsimd.tensor_scalar(mneg[:, :, 0:2], src[:, :, 0:5:4], -1.0, None, ALU.mult).then_inc(s_neg, 1)
                nc.gpsimd.tensor_scalar(mneg[:, :, 2:4], src[:, :, 5:7], -1.0, None, ALU.mult).then_inc(s_neg, 1)
                pwait(s_mw, 16 * s)
                pwait(s_neg, n + 2)
                nc.gpsimd.tensor_copy(msplit[:, 0], mneg[:, :, :]).then_inc(s_neg, 1)
                pwait(s_neg, n + 3)
                nc.gpsimd.tensor_tensor(mrest[:, :, :], mneg[:, :, :], msplit[:, 0], ALU.subtract).then_inc(s_neg, 1)
                pwait(s_neg, n + 4)
                nc.gpsimd.tensor_copy(msplit[:, 1], mrest[:, :, :]).then_inc(s_neg, 1)
                pwait(s_neg, n + 5)
                nc.gpsimd.tensor_tensor(msplit[:, 2], mrest[:, :, :], msplit[:, 1], ALU.subtract)\
                    .then_inc(s_neg, 1)

            NG4 = KVH * NI * 2

            def subtract(bb):
                n = 10 * bb
                pwait(s_rl, 2 * bb + 2)
                pwait(s_post, n)
                nc.gpsimd.tensor_tensor(at[:, :, :],
                                        on_s[:, :, :, :, :].rearrange("p k i c v -> p (k i c) v")[:, :, 0:2 * HD],
                                        rl[:, :, :, :].rearrange("p k i c -> p (k i c)").unsqueeze(2)
                                        .to_broadcast([P, 2 * NG4, 2 * HD]), ALU.mult).then_inc(s_post, 1)
                pwait(s_post, n + 1)
                pair = at[:, :, :].rearrange("p (n j) v -> p n j v", j=2)
                nc.gpsimd.tensor_tensor(dif[:, :, :, :, :].rearrange("p k i r v -> p (k i r) v"),
                                        pair[:, :, 0, :], pair[:, :, 1, :], ALU.add)\
                    .then_inc(s_post, 1)
                pwait(s_post, n + 2)
                flat = dif[:, :, :, :, :].rearrange("p k i r v -> p (k i r) v")
                nc.gpsimd.tensor_tensor(sq[:, :, :], flat, flat, ALU.mult).then_inc(s_post, 1)

            def rms_norm(bb):
                n = 10 * bb + 3
                pwait(s_newton, 4 * (bb + 1))
                pwait(s_post, n)
                nc.gpsimd.tensor_tensor(dn[:, :, :, :, :].rearrange("p i k r v -> p k i r v"), dif[:, :, :, :, :],
                                        rinv[:, :].rearrange("p (k i r) -> p k i r", k=KVH, i=NI).unsqueeze(4)
                                        .to_broadcast([P, KVH, NI, 2, 2 * HD]), ALU.mult)\
                    .then_inc(s_post, 1)

            def layer_norm(bb):
                n = 10 * bb + 4
                pwait(s_bn, 8 * bb + 8)
                pwait(s_post, n)
                nc.gpsimd.tensor_scalar(vare[:, :], bag[:, :, 1], LN_EPS, None, ALU.add).then_inc(s_post, 1)
                pwait(s_post, n + 1)
                nc.gpsimd.tensor_tensor(rstd[:, :], vare[:, :], half[:, 0:NI], ALU.pow).then_inc(s_post, 1)
                pwait(s_x1st, 16 * bb)
                for i in range(NI):
                    pwait(s_post, n + 2)
                    nc.gpsimd.tensor_scalar(x1[:, i, :], res[:, i, :], bag[:, i, 0:1], rstd[:, i:i + 1],
                                            ALU.subtract, ALU.mult).then_inc(s_post, 1)

            pool.wait_ge(s_half, 2)
            for a in range(2):
                split(0, a, 2 * a + 2)

            def body(b):
                for p in range(SUPER):
                    for u in range(NU):
                        if on(b, p, 2):
                            mask(b, p, u)
                        if u == 2 and on(b, p, 1):
                            negate(b, p)
                        if u == 17 and p < 2 and used(b, p, "q"):
                            split(b + 1, p, uses_before(b, p, ("q_swap", "k_swap")[p]) + 1)
                        if p == 2 and u == 5 and (not isinstance(b, int) or b < B):
                            pwait(s_free, v_free(b))
                            if isinstance(b, int):
                                wait(pool, s_pv, NG * 4 * b)
                            else:
                                pwait(s_pv, NG * 4 * b)
                            if isinstance(b, int) and b == 0:
                                pool.wait_ge(s_vzero, 2)
                            nc.gpsimd.tensor_copy(v_aug[:, :, :, 0:2 * HD].rearrange("p i k v -> p (i k) v"),
                                                  v_new[:, :, :, :].rearrange("p i k v -> p (i k) v"))\
                                .then_inc(s_vaug, 1)
                        if used(b, p, "wo"):
                            if (p, u) == (2, 12):
                                subtract(b - 1)
                            if (p, u) == (2, 16):
                                rms_norm(b - 1)
                            if (p, u) == (3, 9):
                                layer_norm(b - 1)

            def v_free(b):
                if isinstance(b, int) and b == 0:
                    return len(PREP)
                return uses_before(b - 1, 3, "v") + 1

            iterations(pool, body)

            pool.wait_ge(s_x1st, 16 * B)
            pool.wait_ge(s_pos, 1)
            for n in range(NTILE):
                nc.gpsimd.indirect_dma_start(out=x_sorted, out_offset=bass.IndirectOffsetOnAxis(pos_u[:, n:n + 1], 0),
                                             in_=x1_all[:, n, :], in_offset=None).then_inc(s_scat, 16)
                if n in (0, 1):
                    nc.gpsimd.indirect_dma_start(out=wbuf[:, n, :], out_offset=None, in_=w12,
                                                 in_offset=bass.IndirectOffsetOnAxis(es_u[:, n:n + 1], 0))\
                        .then_inc(s_wg[n], 16)
            for j in range(2, NSLOT):
                pool.wait_ge(s_y, j - 1)
                nc.gpsimd.indirect_dma_start(out=wbuf[:, j % 2, :], out_offset=None, in_=w12,
                                             in_offset=bass.IndirectOffsetOnAxis(es_u[:, j:j + 1], 0))\
                    .then_inc(s_wg[j % 2], 16)
            pool.wait_ge(s_yst[0], 16 * ((NSLOT + 1) // 2))
            pool.wait_ge(s_yst[1], 16 * (NSLOT // 2))
            for n in range(NTILE):
                nc.gpsimd.indirect_dma_start(out=yg[:, n, :], out_offset=None, in_=y_sorted,
                                             in_offset=bass.IndirectOffsetOnAxis(pos_u[:, n:n + 1], 0))\
                    .then_inc(s_yg[n // 4], 16)
            for g in range(NTILE // 4):
                pool.wait_ge(s_st2, 5 * (g + 1))
                sl = slice(4 * g, 4 * g + 4)
                nc.gpsimd.tensor_tensor(rstd2[:, sl], var2[:, sl], half[:, 0:4], ALU.pow).then_inc(s_rs2, 1)

        @block.vector
        def _(dve):
            V = nc.vector
            V.memset(qa[:, :, :].rearrange("p k t -> p (k t)").bitcast(F32), 0.0).then_inc(s_clear, 1)
            V.memset(ka[:, 0:2].rearrange("p c k t -> p (c k t)").bitcast(F32), 0.0).then_inc(s_clear, 1)
            dve.wait_ge(s_const, ALL_CONST)
            V.tensor_tensor(lam_p[:, :, :], lam_s[:, 0:4:2, :], lam_s[:, 1:4:2, :], ALU.mult).then_inc(s_lam, 1)
            dve.wait_ge(s_lam, 1)
            V.tensor_reduce(lam_d[:, 0:2], lam_p[:, :, :], AX.X, ALU.add).then_inc(s_lam, 1)
            dve.wait_ge(s_lexp, 1)
            V.tensor_scalar(lam_n[:, :], lam_d[:, 3:4], lam_d[:, 2:3], -LAMBDA_INIT, ALU.subtract, ALU.add)\
                .then_inc(s_lam, 1)
            V.memset(x1_all[:, :, :].rearrange("p n d -> p (n d)"), 0.0).then_inc(s_zero, 1)
            V.tensor_scalar(rms_c[:, :], rms_s[:, :], (1.0 - LAMBDA_INIT) * math.sqrt(2 * HD), None, ALU.mult)\
                .then_inc(s_lam, 1)
            dve.wait_ge(s_lam, 4)
            V.tensor_scalar(wo_n[:, :], wo_s[:, :], rms_c[:, 0:1], None, ALU.mult).then_inc(s_won, 1)

            def rotate(name, n, bn):
                k = PREP.index(name)
                wait(dve, s_split, 10 * bn + 5 * (k // 2) - 4)
                wait(dve, s_misc, n + 1)
                V.tensor_tensor((rot1, rot2)[k % 2][:, :], misc[:, :], rope[:, k, :], ALU.mult)\
                    .then_inc(s_free, 1)

            def row_max(b, p, u):
                kind, kk, c = UNITS[u]
                s = 4 * b + p
                bk = nat_b[u % 3]
                dst = mr[:, p % 2]
                if u == 0:
                    wait(dve, s_neg, 6 * (s - 2) + 2)
                wait(dve, s_nat, NU * s + u + 1)
                if kind == "A":
                    o, i = dst[:, 2 * c + kk, 6:7], bk[:, :]
                elif kind == "B":
                    o, i = dst[:, 2 * c + kk, 0:4], bk[:, :].rearrange("p (n t) -> p n t", t=P)
                else:
                    o, i = dst[:, 2 * c:2 * c + 2, 4], bk[:, :].rearrange("p (n t) -> p n t", n=2)
                V.tensor_reduce(o, i, AX.X, ALU.max).then_inc(s_max, 1)
                if u == NU - 1:
                    wait(dve, s_max, (NU + 1) * s + NU)
                    V.tensor_reduce(dst[:, :, 5:6], dst[:, :, 1:4], AX.X, ALU.max).then_inc(s_max, 1)

            def take(b, p, u):
                for name in misc_at(b, p, u):
                    if name not in ("q", "q_swap", "k", "k_swap", "wo", "router"):
                        continue
                    n = uses_before(b, p, name)
                    if name == "wo":
                        bb = b - 1
                        wait(dve, s_xn, 16 * (bb + 1))
                        wait(dve, s_post, 10 * bb)
                        wait(dve, s_misc, n + 1)
                        V.tensor_tensor(res[:, :, :], misc[:, :].rearrange("p (i d) -> p i d", i=NI), xn[:, :, :],
                                        ALU.add).then_inc(s_free, 1)
                        wait(dve, s_free, n + 1)
                        for i in range(NI):
                            V.bn_stats(bst[:, i, :], res[:, i, :]).then_inc(s_bn, 1)
                        wait(dve, s_bn, 8 * bb + 4)
                        dve.nop(nofuse=True)
                        for i in range(NI):
                            V.bn_aggr(bag[:, i, :], bst[:, i, :]).then_inc(s_bn, 1)
                    elif name == "router":
                        wait(dve, s_misc, n + 1)
                        V.tensor_tensor(logit[:, bass.ds((b - 1) * NI, NI), :],
                                        misc[:, 0:NI * NX].rearrange("p (i e) -> p i e", i=NI),
                                        rb_s[:, :].unsqueeze(1).to_broadcast([P, NI, NX]), ALU.add)\
                            .then_inc(s_free, 1)
                    else:
                        rotate(name, n, b + 1)

            for n, name in enumerate(PREP[:4]):
                rotate(name, n, 0)

            def body(b):
                for p in range(SUPER):
                    for u in range(NU):
                        if on(b, p, 0):
                            row_max(b, p, u)
                        if u:
                            take(b, p, u - 1)
                        if used(b, p, "wo"):
                            bb = b - 1
                            if (p, u) == (2, 11):
                                wait(dve, s_free, uses_before(b, 2, "sel1") + 1)
                                V.reciprocal(rl[:, :, :, :], on_s[:, :, :, :, 2 * HD]).then_inc(s_rl, 1)
                                wait(dve, s_rl, 2 * bb + 1)
                                second = rl[:, :, :, :].rearrange("p k i (r j) -> p (k i r) j", j=2)[:, :, 1]
                                V.tensor_scalar(second, second, lam_n[:, 0:1], None, ALU.mult).then_inc(s_rl, 1)
                            if (p, u) == (2, 13):
                                wait(dve, s_post, 10 * bb + 3)
                                V.tensor_reduce(ss[:, :], sq[:, :, :], AX.X, ALU.add).then_inc(s_ss, 1)
                            if (p, u) == (2, 15):
                                n = 4 * bb
                                wait(dve, s_ss, bb + 1)
                                wait(dve, s_newton, n)
                                V.tensor_scalar(nv[:, :], ss[:, :], 2 * HD * RMS_EPS, -0.5, ALU.add, ALU.mult)\
                                    .then_inc(s_newton, 1)
                                wait(dve, s_guess, 2 * bb + 2)
                                V.tensor_tensor(ny[:, :], rg[:, :], rg[:, :], ALU.mult).then_inc(s_newton, 1)
                                wait(dve, s_newton, n + 2)
                                V.tensor_tensor(ny[:, :], ny[:, :], nv[:, :], ALU.mult).then_inc(s_newton, 1)
                                wait(dve, s_newton, n + 3)
                                V.scalar_tensor_tensor(rinv[:, :], ny[:, :], 1.5, rg[:, :], ALU.add, ALU.mult)\
                                    .then_inc(s_newton, 1)

            iterations(dve, body)

            E_, D_ = rt, [P, NTILE, NX]
            count = [0]

            def step(ins):
                count[0] += 1
                ins.then_inc(s_route, 1)
                dve.wait_ge(s_route, count[0])

            io_k, io_j = iota[:, 0:16], iota[:, 16:16 + NSLOT]
            io_e, io_p = iota[:, 16 + NSLOT:16 + NSLOT + NX], iota[:, 16 + NSLOT + NX:17 + NSLOT + NX]

            def over(a, shape, axis):
                return a.unsqueeze(axis).to_broadcast(shape)

            dve.wait_ge(s_free, TOTAL_MISC)
            step(V.tensor_reduce(rmax[:, :], logit[:, :, :], AX.X, ALU.max))
            step(V.tensor_tensor(E_["d"][:, :, :], logit[:, :, :], over(rmax[:, :], D_, 2), ALU.subtract))
            step(V.tensor_tensor(E_["t"][:, :, :], logit[:, :, :], over(rmax[:, :], D_, 2), ALU.is_equal))
            step(V.scalar_tensor_tensor(E_["a"][:, :, :], E_["t"][:, :, :], -float(NX), over(io_e, D_, 1),
                                        ALU.mult, ALU.add))
            step(V.tensor_reduce(rmin[:, :], E_["a"][:, :, :], AX.X, ALU.min))
            dve.wait_ge(s_rexp, 1)
            step(V.tensor_reduce(rsum[:, :], E_["e"][:, :, :], AX.X, ALU.add))
            step(V.reciprocal(maxp[:, :], rsum[:, :]))
            step(V.tensor_copy(E_["z"][:, :, :], E_["a"][:, :, :]))
            step(V.tensor_tensor(E_["oh"][:, :, :], E_["a"][:, :, :], over(rmin[:, :], D_, 2), ALU.is_equal))
            dve.wait_ge(s_rank, 1)
            step(V.tensor_copy(E_["b"][:, :, :], banks[1][:, 0:NTILE * NX].rearrange("p (n e) -> p n e", e=NX)))
            step(V.tensor_copy(E_["a"][:, :, :], E_["b"][:, :, :]))
            cur, nxt, d = "b", "c", 1
            while d < NTILE:
                step(V.tensor_copy(E_[nxt][:, 0:d, :], E_[cur][:, 0:d, :]))
                step(V.tensor_tensor(E_[nxt][:, d:, :], E_[cur][:, d:, :], E_[cur][:, 0:NTILE - d, :], ALU.add))
                cur, nxt, d = nxt, cur, 2 * d
            total = E_[cur][:, NTILE - 1, :]
            cs = [P, NX, 16]
            step(V.tensor_tensor(cmp_n[:, :, :], over(total, cs, 2), over(io_k, cs, 1), ALU.is_gt))
            step(V.tensor_reduce(nsl[:, 0, :], cmp_n[:, :, :], AX.X, ALU.add))
            a = 0
            for d in (1, 2, 4):
                step(V.tensor_copy(nsl[:, a + 1, 0:d], nsl[:, a, 0:d]))
                step(V.tensor_tensor(nsl[:, a + 1, d:], nsl[:, a, d:], nsl[:, a, 0:NX - d], ALU.add))
                a += 1
            step(V.tensor_tensor(nsl[:, 4, :], nsl[:, 3, :], nsl[:, 0, :], ALU.subtract))
            step(V.tensor_scalar(nsl[:, 4, :], nsl[:, 4, :], float(SLOT), None, ALU.mult))
            step(V.tensor_tensor(E_[nxt][:, :, :], E_[cur][:, :, :], E_["a"][:, :, :], ALU.subtract))
            step(V.tensor_tensor(E_["t"][:, :, :], E_[nxt][:, :, :],
                                 banks[0][:, 0:NTILE * NX].rearrange("p (n e) -> p n e", e=NX), ALU.add))
            step(V.tensor_tensor(E_["d"][:, :, :], E_["t"][:, :, :], over(nsl[:, 4, :], D_, 1), ALU.add))
            step(V.tensor_tensor(E_["t"][:, :, :], E_["d"][:, :, :], E_["oh"][:, :, :], ALU.mult))
            step(V.tensor_reduce(pos_f[:, :], E_["t"][:, :, :], AX.X, ALU.add))
            step(V.tensor_copy(pos_u[:, :], pos_f[:, :]))
            ss_ = [P, NSLOT, NX - 1]
            step(V.tensor_tensor(cmp_s[:, :, :], over(nsl[:, 3, 0:NX - 1], ss_, 1), over(io_j, ss_, 2), ALU.is_le))
            step(V.tensor_reduce(es[:, :], cmp_s[:, :, :], AX.X, ALU.add))
            step(V.tensor_scalar(es_r[:, :], es[:, :], float(P), io_p, ALU.mult, ALU.add))
            V.tensor_copy(es_u[:, :], es_r[:, :]).then_inc(s_pos, 1)

            def take_x(j, par):
                wait(dve, s_xturn, j + 1)
                wait(dve, s_h, NF * (j - 1))
                V.tensor_copy(xst[:, par, :], banks[4][:, 0:SLOT]).then_inc(s_xst, 1)

            def gate(j, par):
                for f in range(NF):
                    wait(dve, s_silu, NF * j + f + 1)
                    if f == 0:
                        wait(dve, s_y, j - 1)
                    V.tensor_tensor(u_s[:, par, f, :], sa[:, f, :], banks[f][:, SLOT:2 * SLOT], ALU.mult)\
                        .then_inc(s_u, 1)

            take_x(0, 0)
            gate(0, 0)
            take_x(1, 1)
            gate(1, 1)
            take_x(2, 0)
            gate(2, 0)
            take_x(3, 1)
            with dve.Fori(1, (NSLOT - 1) // 2 - 1) as k:
                gate(2 * k + 1, 1)
                take_x(2 * k + 2, 0)
                gate(2 * k + 2, 0)
                take_x(2 * k + 3, 1)
            gate(NSLOT - 2, 1)
            take_x(NSLOT - 1, 0)
            gate(NSLOT - 1, 0)

            def mix(g):
                dve.wait_ge(s_yg[g], 64)
                for n in range(4 * g, 4 * g + 4):
                    V.scalar_tensor_tensor(yg[:, n, :], yg[:, n, :], maxp[:, n:n + 1], x1_all[:, n, :], ALU.mult,
                                           ALU.add).then_inc(s_res, 1)
                dve.wait_ge(s_res, 4 * g + 4)
                for n in range(4 * g, 4 * g + 4):
                    V.bn_stats(bst2[:, n, :], yg[:, n, :]).then_inc(s_bn, 1)
                dve.wait_ge(s_bn, 8 * B + 4 * g + 4)
                for n in range(4 * g, 4 * g + 4):
                    V.bn_aggr(bag2[:, n, :], bst2[:, n, :]).then_inc(s_st2, 1)
                dve.wait_ge(s_st2, 5 * g + 4)
                V.tensor_scalar(var2[:, 4 * g:4 * g + 4], bag2[:, 4 * g:4 * g + 4, 1], LN_EPS, None, ALU.add)\
                    .then_inc(s_st2, 1)

            def scale(g):
                dve.wait_ge(s_rs2, g + 1)
                for n in range(4 * g, 4 * g + 4):
                    V.tensor_scalar(yg[:, n, :], yg[:, n, :], bag2[:, n, 0:1], rstd2[:, n:n + 1], ALU.subtract,
                                    ALU.mult).then_inc(s_fin, 1)

            for g in range(NTILE // 4):
                mix(g)
                if g:
                    scale(g - 1)
            scale(NTILE // 4 - 1)


def kernel(L0_attn_x, L0_attn_Wq, L0_attn_Wk, L0_attn_Wv, L0_attn_Wo, L0_attn_lambda_q1, L0_attn_lambda_k1,
           L0_attn_lambda_q2, L0_attn_lambda_k2, L0_attn_rms_w, L0_ffn_router_w, L0_ffn_router_b, L0_ffn_w1,
           L0_ffn_w2):
    import ml_dtypes
    import concourse.bacc as bacc
    from concourse.bass_utils import run_bass_kernel_spmd

    f = np.float32
    x = np.ascontiguousarray(L0_attn_x).reshape(B * T, E)
    r, j, d, kv = np.meshgrid(range(2), range(2), range(HD), range(KVH), indexing="ij")
    q_col = (((2 * kv + r) * 2 + j) * HD + d).ravel()
    q_swap = (((2 * kv + r) * 2 + j) * HD + (d ^ 2)).ravel()
    k_col = ((kv * 2 + j) * HD + d).ravel()
    k_swap = ((kv * 2 + j) * HD + (d ^ 2)).ravel()
    Wq, Wk, w2 = np.asarray(L0_attn_Wq), np.asarray(L0_attn_Wk), np.asarray(L0_ffn_w2)
    inv_freq = 1.0 / 10000.0 ** (np.arange(0, HD, 2, dtype=f) / HD)
    freqs = np.outer(np.arange(T, dtype=f), inv_freq)
    dd = d.ravel()
    cos = np.cos(freqs).astype(f).T[dd % 2]
    sin = np.sin(freqs).astype(f).T[dd % 2] * np.where(dd < 2, 1, -1)[:, None]
    scale = HD ** -0.5
    rope = np.stack([cos * scale, sin * scale, cos, sin], 1).astype(f)
    pick = np.zeros((P, 4 * VW), f)
    for c in range(4):
        for v in range(VW):
            pick[32 * c + v, c * VW + v] = 1
    before = (np.arange(P)[:, None] < np.arange(P)[None, :]).astype(f)
    iota = np.concatenate([np.arange(16) * SLOT, np.arange(NSLOT), np.arange(NX)]).astype(f)
    iota = np.concatenate([np.broadcast_to(iota, (P, iota.size)), np.arange(P, dtype=f)[:, None]], 1)
    causal = np.where(np.arange(P)[None, :] > np.arange(P)[:, None], MASKED, 0.0)
    arrays = {
        "xT": x.T, "x": x, "wq": Wq[:, q_col], "wqs": Wq[:, q_swap], "wk": Wk[:, k_col], "wks": Wk[:, k_swap],
        "wv": np.asarray(L0_attn_Wv), "wo": np.asarray(L0_attn_Wo),
        "lam": np.concatenate([np.asarray(a) for a in (L0_attn_lambda_q1, L0_attn_lambda_k1, L0_attn_lambda_q2,
                                                       L0_attn_lambda_k2)]),
        "rms": np.tile(np.asarray(L0_attn_rms_w), H)[:, None],
        "router_w": np.asarray(L0_ffn_router_w), "router_b": np.asarray(L0_ffn_router_b),
        "w12": np.concatenate([np.asarray(L0_ffn_w1), w2.reshape(NX, NF, P, E).transpose(0, 2, 1, 3)
                               .reshape(NX, P, NF * E)], 2).reshape(NX * P, 3 * FFN),
        "c_rope": rope, "c_ident": np.eye(P, dtype=f),
        "c_mask": np.concatenate([np.eye(P), causal], 1).astype(ml_dtypes.bfloat16),
        "c_sel": pick, "c_tri": np.stack([before, np.ones((P, P), f)], 1), "c_iota": iota,
        "c_one": np.repeat([1, 0], MROWS)[:, None].repeat(KVH * T, 1).astype(ml_dtypes.bfloat16),
    }
    arrays = {"in_" + k: np.ascontiguousarray(v) for k, v in arrays.items()}
    nc = bacc.Bacc("TRN2", target_bir_lowering=False, num_devices=1)
    args = [nc.dram_tensor(k, v.shape, mybir.dt.from_np(v.dtype), kind="ExternalInput").ap()
            for k, v in arrays.items()]
    args.append(nc.dram_tensor("out_dram", (B * T, E), F32, kind="ExternalOutput").ap())
    build(nc, *args)
    got = run_bass_kernel_spmd(nc, [arrays], core_ids=[0])
    return got.results[0]["out_dram"].reshape(B, T, E)
```

```python
import math
from contextlib import ExitStack

import numpy as np

import concourse.bass as bass
from concourse import mybir

F32 = mybir.dt.float32
BF16 = mybir.dt.bfloat16
U32 = mybir.dt.uint32
I32 = mybir.dt.int32
ALU = mybir.AluOpType
ACT = mybir.ActivationFunctionType
AX = mybir.AxisListType

B, T, E = 8, 512, 128
P = 128
H, KVH = 16, 8
HD = E // H // 2
NI = T // P
NX = 8
FFN = 512
NF = FFN // P
LAMBDA_INIT = 0.8 - 0.6 * math.exp(-0.3 * 12)
RMS_EPS, LN_EPS = 1e-6, 1e-5
MASKED = -1e30

Q_PART = [0, 0, 0, 1, 1, 2]
K_PART = [0, 1, 2, 0, 1, 0]
TERMS = len(Q_PART)
ROWS = TERMS * HD
MROWS = 3
VW = 2 * HD + 1

SUPER = KVH // 2
NS = B * SUPER
UNITS = ([("A", 0, c) for c in range(4)] + [("B", 0, c) for c in range(4)] + [("C", 0, c) for c in range(4)]
         + [("A", 1, c) for c in range(4)] + [("B", 1, c) for c in range(4)])
NU = len(UNITS)
GROUPS = [("A", 0, 0, 3), ("B", 0, 4, 7), ("C", 0, 8, 11), ("A", 1, 12, 15), ("C", 1, 8, 11), ("B", 1, 16, 19)]
NG = len(GROUPS)
LAST_GROUP = [0] * 4 + [1] * 4 + [4] * 4 + [3] * 4 + [5] * 4
PV_AT = {7: 0, 11: 1, 15: 2, 19: 3}
PV_TAIL_AT = {1: 4, 3: 5}

NEWTON = 12

SLOT = 256
NSLOT = B * T // SLOT + NX - 1
NTILE = B * T // P
RING = 4
XW = E + 2

MISC = []
for _p in range(SUPER):
    MISC += [(_p, 1, "sel0"), (_p, 4, "turn_max"), (_p, 10, "sel1")]
MISC += [(0, 13, "q"), (0, 16, "q_swap"), (1, 13, "k"), (1, 16, "k_swap"), (3, 13, "v"),
         (3, 5, "turn_attn"), (3, 7, "wo"), (3, 16, "turn_x1"), (3, 18, "router")]
MISC.sort(key=lambda m: m[:2])
PREP = ["q", "q_swap", "k", "k_swap", "v"]
POST = ["turn_attn", "wo", "turn_x1", "router"]


def back(u):
    return u - 3 if u >= 3 else (-2, -1, -3)[u]


def on(b, p, lag):
    return not isinstance(b, int) or 0 <= SUPER * b + p - lag < NS


def used(b, p, name):
    if not isinstance(b, int):
        return True
    if name in PREP:
        return b + 1 < B
    if name in POST:
        return b >= 1
    return on(b, p, 1 if name == "turn_max" else 3)


def uses_before(b, p, name):
    n = len(PREP)
    whole = b if isinstance(b, int) else 1
    for i in range(whole):
        n += sum(used(i, m[0], m[2]) for m in MISC)
    if not isinstance(b, int):
        n = n + (b - 1) * len(MISC)
    for m in MISC:
        if (m[0], m[2]) == (p, name):
            return n
        n = n + (1 if used(b, m[0], m[2]) else 0)
    raise KeyError(name)


TOTAL_MISC = len(PREP) + sum(used(i, m[0], m[2]) for i in range(B + 1) for m in MISC)


def misc_at(b, p, u):
    return [m[2] for m in MISC if m[:2] == (p, u) and used(b, p, m[2])]


def build(nc, xT, x, wq, wqs, wk, wks, wv, wo, lam, rms, router_w, router_b, w12, c_rope, c_ident, c_mask,
          c_sel, c_tri, c_iota, c_one, c_pad, out):
    with ExitStack() as ctx:
        def sb(name, shape, dt=F32):
            return ctx.enter_context(nc.sbuf_tensor(name, shape, dt))

        def bank(name, width=512):
            return ctx.enter_context(nc.psum_tensor(name, [P, width], F32))

        def sem(name):
            return ctx.enter_context(nc.semaphore(name))

        qk_parts = nc.dram_tensor("qk_parts", (B, 2, TERMS, 4, HD, KVH, T), BF16).ap()
        max_rows = nc.dram_tensor("max_rows", (NS, 3, 4, 2 * NI, P), BF16).ap()
        x_sorted = nc.dram_tensor("x_sorted", (NSLOT * SLOT, XW), F32).ap()

        rope = sb("rope", [P, 4, T])
        ident = sb("ident", [P, P])
        ident_b = sb("ident_b", [P, P], BF16)
        mask_b = sb("mask_b", [P, P], BF16)
        sel = sb("sel", [P, 4 * VW])
        tri = sb("tri", [P, 2, P])
        iota = sb("iota", [P, 16 + NSLOT + NX + 1 + NTILE])
        wq_s = sb("wq_s", [P, 4, P])
        wv_s = sb("wv_s", [P, KVH * 2 * HD])
        wo_s = sb("wo_s", [P, P])
        wo_n = sb("wo_n", [P, P])
        lam_s = sb("lam_s", [P, 4, HD])
        lam_p = sb("lam_p", [P, 2, HD])
        lam_d = sb("lam_d", [P, 4])
        lam_n = sb("lam_n", [P, 1])
        rms_s = sb("rms_s", [P, 1])
        rms_c = sb("rms_c", [P, 1])
        rw_s = sb("rw_s", [P, NX])
        rb_s = sb("rb_s", [P, NX])
        half = sb("half", [P, NI])

        xt_s = sb("xt_s", [P, T])
        rot1 = sb("rot1", [P, T])
        rot2 = sb("rot2", [P, T])
        rot = sb("rot", [P, T])
        rest = sb("rest", [P, T])
        parts = sb("parts", [P, 2, 3, T], BF16)
        v_new = sb("v_new", [P, NI, KVH, 2 * HD])
        v_aug = sb("v_aug", [P, NI, KVH, 32])
        qa = sb("qa", [P, KVH, T], BF16)
        ka = sb("ka", [P, 4, KVH, T], BF16)
        mr = sb("mr", [P, 2, 8, 7])
        mneg = sb("mneg", [P, 8, NI])
        mrest = sb("mrest", [P, 8, NI])
        msplit = sb("msplit", [P, 3, 8, NI], BF16)
        mturn = sb("mturn", [96, P], BF16)
        prob = sb("prob", [P, NU, T])
        ot = sb("ot", [P, 2, T])
        on_s = sb("on_s", [P, KVH, NI, 4, VW])
        rl = sb("rl", [P, KVH, NI, 4])
        at = sb("at", [P, KVH * NI * 4, 2 * HD])
        dif = sb("dif", [P, KVH, NI, 2, 2 * HD])
        sq = sb("sq", [P, KVH * NI * 2, 2 * HD])
        ss = sb("ss", [P, KVH * NI * 2])
        nint = sb("nint", [P, KVH * NI * 2], I32)
        nv = sb("nv", [P, KVH * NI * 2])
        ny = sb("ny", [P, KVH * NI * 2])
        rinv = sb("rinv", [P, KVH * NI * 2])
        dn = sb("dn", [P, NI, KVH, 2, 2 * HD])
        dt_s = sb("dt_s", [P, T])
        xn = sb("xn", [P, NI, E])
        res = sb("res", [P, NI, E])
        bst = sb("bst", [P, NI, 6])
        bag = sb("bag", [P, NI, 2])
        vare = sb("vare", [P, NI])
        rstd = sb("rstd", [P, NI])
        shift = sb("shift", [P, NI])
        x1 = sb("x1", [P, NI, E])
        x1t = sb("x1t", [P, T])
        x1_all = sb("x1_all", [P, NTILE, XW])
        logit = sb("logit", [P, NTILE, NX])

        rt = {n: sb("rt_" + n, [P, NTILE, NX]) for n in ("d", "e", "t", "oh", "a", "b", "c", "z")}
        rmax = sb("rmax", [P, NTILE])
        rsum = sb("rsum", [P, NTILE])
        rmin = sb("rmin", [P, NTILE])
        pos_f = sb("pos_f", [P, NTILE])
        pos_u = sb("pos_u", [P, NTILE], U32)
        cmp_n = sb("cmp_n", [P, NX, 16])
        nsl = sb("nsl", [P, 5, NX])
        cmp_s = sb("cmp_s", [P, NSLOT, NX - 1])
        es = sb("es", [P, NSLOT])
        es_r = sb("es_r", [P, NSLOT])
        es_u = sb("es_u", [P, NSLOT], U32)
        wbuf = prob[:, NU - RING * 3 * FFN // T:, :].rearrange("p (n h) t -> p n (h t)", n=RING)
        xs = sb("xs", [P, RING, SLOT // P, XW])
        xst = sb("xst", [P, 2, SLOT])
        sa = sb("sa", [P, NF, SLOT])
        u_s = sb("u_s", [P, 2, NF, SLOT])
        row_u = sb("row_u", [P, RING, SLOT // P], U32)
        ymix = sb("ymix", [P, 2, SLOT // P, E])
        ynorm = sb("ynorm", [P, 2, SLOT // P, E])
        bst2 = sb("bst2", [P, SLOT // P, 6])
        bag2 = sb("bag2", [P, 2, SLOT // P, 2])
        var2 = sb("var2", [P, 2, SLOT // P])
        rstd2 = sb("rstd2", [P, 2, SLOT // P])
        shift2 = sb("shift2", [P, 2, SLOT // P])

        banks = [bank(f"bank{i}") for i in range(8)]
        nat_b, st_b, pv_b, misc = banks[0:3], banks[3:6], banks[6], banks[7]

        s_const = sem("s_const")
        s_xt = sem("s_xt")
        s_xn = sem("s_xn")
        s_half = sem("s_half")
        s_vzero = sem("s_vzero")
        s_lam = sem("s_lam")
        s_lexp = sem("s_lexp")
        s_won = sem("s_won")
        s_split = sem("s_split")
        s_part = sem("s_part")
        s_written = [sem("s_written_q"), sem("s_written_k")]
        s_vaug = sem("s_vaug")
        s_qk = [sem(f"s_qk{i}") for i in range(SUPER)]
        s_nat = sem("s_nat")
        s_max = sem("s_max")
        s_neg = sem("s_neg")
        s_mw = sem("s_mw")
        s_mrow = [sem(f"s_mrow{i}") for i in range(SUPER)]
        s_st = sem("s_st")
        s_exp = sem("s_exp")
        s_masked = sem("s_masked")
        s_pv = sem("s_pv")
        s_ot = sem("s_ot")
        s_misc = sem("s_misc")
        s_free = sem("s_free")
        s_rl = sem("s_rl")
        s_post = sem("s_post")
        s_ss = sem("s_ss")
        s_newton = sem("s_newton")
        s_bn = sem("s_bn")
        s_x1 = sem("s_x1")
        s_x1st = sem("s_x1st")
        s_clear = sem("s_clear")
        s_ones = sem("s_ones")
        s_xzero = sem("s_xzero")
        s_route = sem("s_route")
        s_rexp = sem("s_rexp")
        s_rank = sem("s_rank")
        s_pos = sem("s_pos")
        s_scat = sem("s_scat")
        s_wg = [sem(f"s_wg{i}") for i in range(RING)]
        s_xs = [sem(f"s_xs{i}") for i in range(RING)]
        s_xturn = sem("s_xturn")
        s_xst = sem("s_xst")
        s_h = sem("s_h")
        s_silu = sem("s_silu")
        s_u = sem("s_u")
        s_y = sem("s_y")
        s_ln = sem("s_ln")
        s_rs2 = sem("s_rs2")
        s_norm = sem("s_norm")
        s_outs = [sem("s_outs0"), sem("s_outs1")]

        block = ctx.enter_context(nc.Block())

        LN_STEPS = 8
        STEADY = NSLOT // RING

        def slots(eng, body):
            for j in range(2 * RING):
                body(j, j // RING, j % RING)
            with eng.Fori(2, STEADY) as k:
                for n in range(RING):
                    body(RING * k + n, k, n)
            for n in range(NSLOT - RING * STEADY):
                body(RING * STEADY + n, STEADY, n)

        def iterations(eng, body):
            body(0)
            body(1)
            with eng.Fori(2, B - 1) as b:
                body(b)
            body(B - 1)
            body(B)

        def wait(eng, s, n):
            if not isinstance(n, int) or n > 0:
                eng.wait_ge(s, n)

        consts = [(wq_s[:, 0, :], wq), (wq_s[:, 1, :], wqs), (wq_s[:, 2, :], wk), (wq_s[:, 3, :], wks),
                  (wv_s[:, :], wv), (rope[:, :, :], c_rope), (ident[:, :], c_ident), (wo_s[:, :], wo),
                  (sel[:, :], c_sel), (tri[:, :, :], c_tri), (iota[:, :], c_iota),
                  (ident_b[:, :], c_mask[:, 0:P]), (mask_b[:, :], c_mask[:, P:2 * P]),
                  (lam_s[:, :, :].rearrange("p a d -> p (a d)"), lam.partition_broadcast(P)),
                  (rw_s[:, :], router_w), (rms_s[:, :], rms), (rb_s[:, :], router_b.partition_broadcast(P))]
        ALL_CONST = 16 * len(consts)
        ones_of = [(ka[32 * c + ROWS:32 * c + ROWS + MROWS, c, :, :].rearrange("p k t -> p (k t)"), c_one[0:MROWS])
                   for c in range(4)]

        @block.sync
        def _(sp):
            def write_parts(bn, a):
                wait(sp, s_split, 6 * bn + 3 * a + 3)
                for term, part in enumerate((Q_PART, K_PART)[a]):
                    sp.dma_start(qk_parts[bn, a, term].rearrange("c d k t -> (c d k) t"),
                                 parts[:, a, part, :]).then_inc(s_written[a], 16)

            def load_slot(bn, q):
                for c in range(4):
                    sp.dma_start(qa[32 * c + ROWS:32 * c + ROWS + MROWS, 2 * q:2 * q + 2, :]
                                 .rearrange("p k t -> p (k t)"), c_one[MROWS:, 0:2 * T]).then_inc(s_qk[q], 16)
                if q == 0:
                    for a in range(2):
                        wait(sp, s_written[a], 16 * TERMS * (bn + 1))
                for c in range(4):
                    for a, dst in enumerate((qa, ka[:, c])):
                        sp.dma_start(dst[32 * c:32 * c + ROWS, 2 * q:2 * q + 2, :].rearrange("p k t -> p (k t)"),
                                     qk_parts[bn, a, :, c, :, 2 * q:2 * q + 2, :].rearrange("r d k t -> r d (k t)"))\
                            .then_inc(s_qk[q], 16)

            sp.dma_start(xt_s[:, :], xT[:, 0:T]).then_inc(s_xt, 16)
            for dst, src in consts:
                sp.dma_start(dst, src).then_inc(s_const, 16)
            sp.dma_start(xn[:, :, :], x[0:T, :].rearrange("(i p) d -> p i d", p=P)).then_inc(s_xn, 16)
            sp.wait_ge(s_clear, 3)
            for dst, src in ones_of:
                sp.dma_start(dst, src).then_inc(s_ones, 16)
            for a in range(2):
                write_parts(0, a)
            load_slot(0, 0)
            sp.wait_ge(s_free, len(PREP))
            sp.dma_start(xt_s[:, :], xT[:, T:2 * T]).then_inc(s_xt, 16)
            for q in range(1, SUPER):
                load_slot(0, q)
            sp.dma_start(x_sorted, c_pad).then_inc(s_xzero, 16)
            sp.wait_ge(s_xzero, 16)

            def body(b):
                for p in range(SUPER):
                    nxt = 4 * b + p + 1
                    if isinstance(b, int):
                        load = SUPER <= nxt < NS
                    else:
                        load = True
                    if load:
                        wait(sp, s_st, NU * (nxt - SUPER + 1))
                        load_slot(b + (p + 1) // SUPER, (p + 1) % SUPER)
                    if on(b, p, 1):
                        s = 4 * b + p - 1
                        q = (p + 3) % SUPER
                        wait(sp, s_free, uses_before(b, p, "turn_max") + 1)
                        sp.dma_start(max_rows[s].rearrange("k c i t -> (k c i) t"), mturn[:, :]).then_inc(s_mw, 16)
                        wait(sp, s_mw, 16 * (s + 1))
                        for c in range(4):
                            sp.dma_start(qa[32 * c + ROWS:32 * c + ROWS + MROWS, 2 * q:2 * q + 2, :]
                                         .rearrange("p k t -> p (k t)"),
                                         max_rows[s, :, c].rearrange("k i t -> k (i t)")).then_inc(s_mrow[q], 16)
                    if used(b, 0, "q") and p in (1, 2):
                        write_parts(b + 1, p - 1)
                    if p == 3 and (not isinstance(b, int) or b + 2 < B):
                        wait(sp, s_free, uses_before(b, 3, "v") + 1)
                        sp.dma_start(xt_s[:, :], xT[:, bass.ds((b + 2) * T, T)]).then_inc(s_xt, 16)
                    if p == 3 and used(b, 3, "wo"):
                        bb = b - 1
                        wait(sp, s_free, uses_before(b, 3, "wo") + 1)
                        if not isinstance(b, int) or b < B:
                            sp.dma_start(xn[:, :, :], x[bass.ds(b * T, T), :].rearrange("(i p) d -> p i d", p=P))\
                                .then_inc(s_xn, 16)
                        wait(sp, s_x1, 4 * bb + 4)
                        sp.dma_start(x1_all[:, bass.ds(bb * NI, NI), 0:E], x1[:, :, :]).then_inc(s_x1st, 16)

            body(0)
            body(1)
            with sp.Fori(2, B - 2) as b:
                body(b)
            body(B - 2)
            body(B - 1)
            body(B)
            sp.wait_ge(s_scat, 16 * NTILE)
            for j in range(NSLOT):
                wait(sp, s_ln, LN_STEPS * (j - RING) + 3)
                sp.dma_start(xs[:, j % RING, :, :], x_sorted[j * SLOT:(j + 1) * SLOT, :]
                             .rearrange("(a p) d -> p a d", p=P)).then_inc(s_xs[j % RING], 16)
            for par in range(2):
                sp.wait_ge(s_outs[par], 32 * ((NSLOT + 1 - par) // 2))

        @block.tensor
        def _(pe):
            def misc_wait(b, p, name):
                n = name if isinstance(name, int) else uses_before(b, p, name)
                wait(pe, s_free, n)

            def prep(name, bn, b=None, p=None):
                misc_wait(b, p, name if b is not None else PREP.index(name))
                if name == "q":
                    wait(pe, s_xt, 16 * (bn + 1))
                if name == "v":
                    for i in range(NI):
                        mm_ = pe.matmul(misc[:, 64 * i:64 * i + 64], xt_s[:, i * P:(i + 1) * P], wv_s[:, :],
                                        start=True, stop=True)
                else:
                    mm_ = pe.matmul(misc[:, :], wq_s[:, PREP.index(name), :], xt_s[:, :], start=True, stop=True)
                mm_.then_inc(s_misc, 1)

            def nat(b, p, u):
                kind, kk, c = UNITS[u]
                s = 4 * b + p
                bk = nat_b[u % 3]
                if u == 0:
                    wait(pe, s_qk[p], 16 * 12 * (b + 1))
                wait(pe, s_max, (NU + 1) * s + back(u) + (1 if u >= 3 else 0))

                def q(kv, i):
                    return qa[:, kv, i * P:(i + 1) * P]

                if kind == "A":
                    pe.matmul(bk[:, :], q(2 * p + kk, 3), ka[:, c, 2 * p + kk, :], start=True, stop=True)
                    m = pe.matmul(bk[:, 384:512], ident_b[:, :], mask_b[:, :], start=False, stop=True,
                                  skip_group_check=True)
                elif kind == "B":
                    pe.matmul(bk[:, 0:128], q(2 * p + kk, 0), ka[:, c, 2 * p + kk, 0:128], start=True, stop=True)
                    pe.matmul(bk[:, 128:512], q(2 * p + kk, 2), ka[:, c, 2 * p + kk, 0:384], start=False, stop=True,
                              skip_group_check=True)
                    pe.matmul(bk[:, 0:128], ident_b[:, :], mask_b[:, :], start=False, stop=True,
                              skip_group_check=True)
                    m = pe.matmul(bk[:, 384:512], ident_b[:, :], mask_b[:, :], start=False, stop=True,
                                  skip_group_check=True)
                else:
                    for h in range(2):
                        pe.matmul(bk[:, 256 * h:256 * h + 256], q(2 * p + h, 1), ka[:, c, 2 * p + h, 0:256],
                                  start=h == 0, stop=True, skip_group_check=h == 1)
                    for h in range(2):
                        m = pe.matmul(bk[:, 256 * h + 128:256 * h + 256], ident_b[:, :], mask_b[:, :], start=False,
                                      stop=True, skip_group_check=True)
                m.then_inc(s_nat, 1)

            def st(b, p, u):
                kind, kk, c = UNITS[u]
                s, q = 4 * b + p - 2, (p + 2) % SUPER
                bk = st_b[u % 3]
                if u == 0:
                    wait(pe, s_mrow[q], 16 * 4 * (b + (1 if p >= 2 else 0)))
                wait(pe, s_exp, NU * s + back(u) + 1)

                def k(kv, j):
                    return ka[:, c, kv, j * P:(j + 1) * P]

                if kind == "A":
                    m = pe.matmul(bk[:, :], k(2 * q + kk, 0), qa[:, 2 * q + kk, :], start=True, stop=True)
                elif kind == "B":
                    pe.matmul(bk[:, 0:384], k(2 * q + kk, 1), qa[:, 2 * q + kk, 128:512], start=True, stop=True)
                    m = pe.matmul(bk[:, 384:512], k(2 * q + kk, 3), qa[:, 2 * q + kk, 384:512], start=False,
                                  stop=True, skip_group_check=True)
                else:
                    for h in range(2):
                        m = pe.matmul(bk[:, 256 * h:256 * h + 256], k(2 * q + h, 2), qa[:, 2 * q + h, 256:512],
                                      start=h == 0, stop=True, skip_group_check=h == 1)
                m.then_inc(s_st, 1)

            def pv(s, g, first_of_batch, batch):
                kind, kk, u0, u1 = GROUPS[g]
                q = s[1]
                wait(pe, s_masked, NU * s[0] + u1 + 1)
                if g == 0:
                    wait(pe, s_ot, 2 * s[0])
                    if first_of_batch:
                        wait(pe, s_vaug, batch + 1)
                if g == 3:
                    wait(pe, s_ot, 2 * s[0] + 1)
                kv = 2 * q + kk
                spans = {"A": [(0, 0, 0)], "B": [(1, 128, 0), (3, 384, 384)], "C": [(2, 256, 256 * kk)]}[kind]
                for n, (j, t0, col) in enumerate(spans):
                    for c in range(4):
                        m = pe.matmul(pv_b[32 * c:32 * c + 32, t0:T], v_aug[:, j, kv, :],
                                      prob[:, u0 + c, col:col + T - t0], start=kind == "A",
                                      stop=True, skip_group_check=True)
                m.then_inc(s_pv, 1)

            def uses(b, p, u):
                for name in misc_at(b, p, u):
                    s = 4 * b + p - 3
                    if name in PREP:
                        prep(name, b + 1, b, p)
                        continue
                    misc_wait(b, p, name)
                    if name in ("sel0", "sel1"):
                        kk = int(name[3])
                        wait(pe, s_ot, 2 * s + kk + 1)
                        for i in range(NI):
                            m = pe.matmul(misc[:, 4 * VW * i:4 * VW * (i + 1)], ot[:, kk, i * P:(i + 1) * P],
                                          sel[:, :], start=True, stop=True)
                    elif name == "turn_max":
                        wait(pe, s_neg, 6 * (4 * b + p))
                        m = pe.transpose(misc[0:96, 0:P // 2].bitcast(BF16),
                                         msplit[:, :, :, :].rearrange("p k c i -> p (k c i)"), ident_b[:, :])
                    elif name == "turn_attn":
                        wait(pe, s_post, 7 * (b - 1) + 4)
                        for i in range(NI):
                            m = pe.transpose(misc[:, i * P:(i + 1) * P],
                                             dn[:, i, :, :, :].rearrange("p k r v -> p (k r v)"), ident[:, :])
                    elif name == "wo":
                        for i in range(NI):
                            m = pe.matmul(misc[:, i * P:(i + 1) * P], dt_s[:, i * P:(i + 1) * P], wo_n[:, :],
                                          start=True, stop=True)
                    elif name == "turn_x1":
                        wait(pe, s_x1, 4 * (b - 1) + 4)
                        for i in range(NI):
                            m = pe.transpose(misc[:, i * P:(i + 1) * P], x1[:, i, :], ident[:, :])
                    elif name == "router":
                        for i in range(NI):
                            m = pe.matmul(misc[:, i * NX:(i + 1) * NX], x1t[:, i * P:(i + 1) * P], rw_s[:, :],
                                          start=True, stop=True)
                    m.then_inc(s_misc, 1)

            pe.wait_ge(s_const, ALL_CONST)
            for name in PREP:
                prep(name, 0)
            pe.wait_ge(s_won, 1)
            pe.wait_ge(s_ones, 64)

            def body(b):
                for p in range(SUPER):
                    for u in range(NU):
                        if on(b, p, 0):
                            nat(b, p, u)
                        if on(b, p, 2):
                            st(b, p, u)
                            if u in PV_AT:
                                pv((4 * b + p - 2, (p + 2) % SUPER), PV_AT[u], p == 2, b)
                        if on(b, p, 3) and u in PV_TAIL_AT:
                            pv((4 * b + p - 3, (p + 1) % SUPER), PV_TAIL_AT[u], False, None)
                        uses(b, p, u)

            iterations(pe, body)

            pe.wait_ge(s_route, 10)
            oh = rt["oh"][:, :, :].rearrange("p n e -> p (n e)")
            pe.matmul(banks[0][:, 0:NTILE * NX], tri[:, 0, :], oh, start=True, stop=True)
            pe.matmul(banks[1][:, 0:NTILE * NX], tri[:, 1, :], oh, start=True, stop=True).then_inc(s_rank, 1)

            def turn_x(j, k, n):
                wait(pe, s_xs[n], 16 * (k + 1))
                wait(pe, s_xst, j)
                for a in range(SLOT // P):
                    m = pe.transpose(banks[4][:, a * P:(a + 1) * P], xs[:, n, a, 0:E], ident[:, :])
                m.then_inc(s_xturn, 1)

            def hidden(j, k, n):
                wait(pe, s_xst, j + 1)
                wait(pe, s_wg[n], 16 * (k + 1))
                for f in range(NF):
                    wait(pe, s_u, NF * (j - 1) + f + 1)
                    for h in range(2):
                        m = pe.matmul(banks[f][:, h * SLOT:(h + 1) * SLOT],
                                      wbuf[:, n, h * FFN + f * P:h * FFN + (f + 1) * P], xst[:, n % 2, :],
                                      start=h == 0, stop=True, skip_group_check=h == 1)
                    m.then_inc(s_h, 1)

            def down(j, n):
                wait(pe, s_u, NF * (j + 1))
                wait(pe, s_ln, LN_STEPS * (j - 2) + 3)
                for a in range(SLOT // P):
                    for f in range(NF):
                        m = pe.matmul(banks[5 + n % 2][:, a * P:(a + 1) * P],
                                      u_s[:, n % 2, f, a * P:(a + 1) * P],
                                      wbuf[:, n, 2 * FFN + f * P:2 * FFN + (f + 1) * P],
                                      start=f == 0, stop=f == NF - 1)
                m.then_inc(s_y, 1)

            def slot(j, k, n):
                hidden(j, k, n)
                if not isinstance(j, int) or j + 1 < NSLOT:
                    turn_x(j + 1, k + (n + 1) // RING, (n + 1) % RING)
                if not isinstance(j, int) or j >= 1:
                    down(j - 1, (n - 1) % RING)

            pe.wait_ge(s_pos, 1)
            turn_x(0, 0, 0)
            slots(pe, slot)
            down(NSLOT - 1, (NSLOT - 1) % RING)

        @block.scalar
        def _(act):
            act.wait_ge(s_lam, 2)
            nc.scalar.activation(lam_d[:, 2:4], lam_d[:, 0:2], ACT.Exp).then_inc(s_lexp, 1)

            def exp(b, p, u):
                s = 4 * b + p - 2
                wait(act, s_st, NU * s + u + 1)
                wait(act, s_pv, NG * (s - 1) + LAST_GROUP[u] + 1)
                nc.scalar.activation(prob[:, u, :], st_b[u % 3][:, :], ACT.Exp).then_inc(s_exp, 1)

            def take_v(n):
                act.wait_ge(s_misc, n + 1)
                nc.scalar.activation(v_new[:, :, :, :].rearrange("p i k v -> p (i k v)"), misc[:, 0:256],
                                     ACT.Copy).then_inc(s_free, 1)

            def take(b, p, u):
                for name in misc_at(b, p, u):
                    if name not in ("sel0", "sel1", "turn_max", "turn_attn", "turn_x1", "v"):
                        continue
                    n = uses_before(b, p, name)
                    if name == "v":
                        wait(act, s_vaug, b + 1)
                        take_v(n)
                        continue
                    if name == "turn_max":
                        wait(act, s_mw, 16 * (4 * b + p - 1))
                    if name in ("sel0", "sel1"):
                        s = 4 * b + p - 3
                        q = (p + 1) % SUPER
                        if q == 0 and name == "sel0":
                            wait(act, s_post, 7 * (b - 1) + 1)
                        wait(act, s_misc, n + 1)
                        nc.scalar.activation(on_s[:, 2 * q + int(name[3]), :, :, :]
                                             .rearrange("p i c v -> p (i c v)"), misc[:, 0:NI * 4 * VW],
                                             ACT.Copy).then_inc(s_free, 1)
                        continue
                    wait(act, s_misc, n + 1)
                    if name == "turn_max":
                        dst, src = mturn[:, :], misc[0:96, 0:P // 2].bitcast(BF16)
                    elif name == "turn_attn":
                        dst, src = dt_s[:, :], misc[:, :]
                    else:
                        dst, src = x1t[:, :], misc[:, :]
                    nc.scalar.activation(dst, src, ACT.Copy).then_inc(s_free, 1)

            def take_ot(s, kk):
                wait(act, s_pv, NG * s + (3 if kk == 0 else 6))
                nc.scalar.activation(ot[:, kk, :], pv_b[:, :], ACT.Copy).then_inc(s_ot, 1)

            def part(bn, a, k):
                wait(act, s_split, 6 * bn + 3 * a + k + 1)
                wait(act, s_written[a], 16 * TERMS * bn)
                nc.scalar.activation(parts[:, a, k, :], (rot, rest)[k][:, :], ACT.Copy).then_inc(s_part, 1)

            for a in range(2):
                part(0, a, 0)
                part(0, a, 1)
            take_v(4)

            def body(b):
                for p in range(SUPER):
                    for u in range(NU):
                        if on(b, p, 2):
                            exp(b, p, u)
                            if u == 16:
                                take_ot(4 * b + p - 2, 0)
                        if on(b, p, 3) and u == 3:
                            take_ot(4 * b + p - 3, 1)
                        if u:
                            take(b, p, u - 1)
                        if used(b, p, "q") and p in (1, 2) and u in (3, 7):
                            part(b + 1, p - 1, u // 7)
                        if used(b, p, "wo") and (p, u) == (3, 12):
                            bb = b - 1
                            wait(act, s_post, 7 * bb + 7)
                            wait(act, s_x1st, 16 * bb)
                            for i in range(NI):
                                nc.scalar.activation(x1[:, i, :], res[:, i, :], ACT.Identity, bias=shift[:, i:i + 1],
                                                     scale=rstd[:, i:i + 1]).then_inc(s_x1, 1)

            iterations(act, body)

            act.wait_ge(s_route, 2)
            nc.scalar.activation(rt["e"][:, :, :].rearrange("p n e -> p (n e)"),
                                 rt["d"][:, :, :].rearrange("p n e -> p (n e)"), ACT.Exp).then_inc(s_rexp, 1)

            def normalise(j, k, n):
                wait(act, s_rs2, 3 * (j + 1))
                wait(act, s_outs[n % 2], 32 * (2 * k + n // 2))
                for a in range(SLOT // P):
                    nc.scalar.activation(ynorm[:, n % 2, a, :], ymix[:, n % 2, a, :], ACT.Identity,
                                         bias=shift2[:, n % 2, a:a + 1],
                                         scale=rstd2[:, n % 2, a:a + 1]).then_inc(s_norm, 1)

            def slot(j, k, n):
                for f in range(NF):
                    wait(act, s_h, NF * j + f + 1)
                    wait(act, s_u, NF * (j - 1) + f + 1)
                    nc.scalar.activation(sa[:, f, :], banks[f][:, 0:SLOT], ACT.Silu).then_inc(s_silu, 1)
                if not isinstance(j, int) or j >= 2:
                    normalise(j - 2, k - (n < 2), (n - 2) % RING)

            slots(act, slot)
            for j in (NSLOT - 2, NSLOT - 1):
                normalise(j, j // RING, j % RING)

        @block.gpsimd
        def _(pool):
            def pwait(s, n):
                wait(pool, s, n)
                if not isinstance(n, int):
                    pool.nop(nofuse=True)

            pool.memset(ka[:, 2:4].rearrange("p c k t -> p (c k t)").bitcast(F32), 0.0).then_inc(s_clear, 1)
            pool.memset(half[:, :], -0.5).then_inc(s_half, 1)
            pool.memset(v_aug[:, :, :, :].rearrange("p i k v -> p (i k v)"), 0.0).then_inc(s_vzero, 1)
            pool.wait_ge(s_vzero, 1)
            pool.memset(v_aug[:, :, :, 2 * HD:VW].rearrange("p i k v -> p (i k) v"), 1.0).then_inc(s_vzero, 1)

            def add(bn, a, n_free):
                pwait(s_free, n_free)
                pwait(s_split, 6 * bn + 3 * a)
                nc.gpsimd.tensor_tensor(rot[:, :], rot1[:, :], rot2[:, :], ALU.add).then_inc(s_split, 1)

            def rest_of(bn, a, k):
                pwait(s_part, 4 * bn + 2 * a + k + 1)
                pwait(s_split, 6 * bn + 3 * a + k + 1)
                if k == 0:
                    nc.gpsimd.tensor_tensor(rest[:, :], rot[:, :], parts[:, a, 0, :], ALU.subtract)\
                        .then_inc(s_split, 1)
                else:
                    pwait(s_written[a], 16 * TERMS * bn)
                    nc.gpsimd.tensor_tensor(parts[:, a, 2, :], rest[:, :], parts[:, a, 1, :], ALU.subtract)\
                        .then_inc(s_split, 1)

            def mask(b, p, u):
                kind = UNITS[u][0]
                s = 4 * b + p - 2
                pwait(s_exp, NU * s + u + 1)
                if kind == "A":
                    v, pattern = prob[:, u, 0:P], [[1, P]]
                elif kind == "B":
                    v = prob[:, u, :].rearrange("p (n t) -> p n t", t=P)[:, 0:4:3, :]
                    pattern = [[0, 2], [1, P]]
                else:
                    v = prob[:, u, :].rearrange("p (n t) -> p n t", t=P)[:, 0:4:2, :]
                    pattern = [[0, 2], [1, P]]
                nc.gpsimd.affine_select(out=v, in_=v, compare_op=ALU.is_ge, fill=0.0, base=0, pattern=pattern,
                                        channel_multiplier=-1).then_inc(s_masked, 1)

            def negate(b, p):
                s = 4 * b + p - 1
                par = (p + 1) % 2
                n = 6 * s
                src = mr[:, par]
                pwait(s_max, (NU + 1) * (s + 1))
                pwait(s_neg, n)
                nc.gpsimd.tensor_scalar(mneg[:, :, 0:2], src[:, :, 0:5:4], -1.0, None, ALU.mult).then_inc(s_neg, 1)
                nc.gpsimd.tensor_scalar(mneg[:, :, 2:4], src[:, :, 5:7], -1.0, None, ALU.mult).then_inc(s_neg, 1)
                pwait(s_mw, 16 * s)
                pwait(s_neg, n + 2)
                nc.gpsimd.tensor_copy(msplit[:, 0], mneg[:, :, :]).then_inc(s_neg, 1)
                pwait(s_neg, n + 3)
                nc.gpsimd.tensor_tensor(mrest[:, :, :], mneg[:, :, :], msplit[:, 0], ALU.subtract).then_inc(s_neg, 1)
                pwait(s_neg, n + 4)
                nc.gpsimd.tensor_copy(msplit[:, 1], mrest[:, :, :]).then_inc(s_neg, 1)
                pwait(s_neg, n + 5)
                nc.gpsimd.tensor_tensor(msplit[:, 2], mrest[:, :, :], msplit[:, 1], ALU.subtract)\
                    .then_inc(s_neg, 1)

            NG4 = KVH * NI * 2

            def over_total(bb):
                pwait(s_rl, 2 * bb + 2)
                pwait(s_post, 7 * bb)
                nc.gpsimd.tensor_tensor(at[:, :, :],
                                        on_s[:, :, :, :, :].rearrange("p k i c v -> p (k i c) v")[:, :, 0:2 * HD],
                                        rl[:, :, :, :].rearrange("p k i c -> p (k i c)").unsqueeze(2)
                                        .to_broadcast([P, 2 * NG4, 2 * HD]), ALU.mult).then_inc(s_post, 1)

            def difference(bb):
                pwait(s_post, 7 * bb + 1)
                pair = at[:, :, :].rearrange("p (n j) v -> p n j v", j=2)
                nc.gpsimd.tensor_tensor(dif[:, :, :, :, :].rearrange("p k i r v -> p (k i r) v"),
                                        pair[:, :, 0, :], pair[:, :, 1, :], ALU.add).then_inc(s_post, 1)

            def square(bb):
                pwait(s_post, 7 * bb + 2)
                flat = dif[:, :, :, :, :].rearrange("p k i r v -> p (k i r) v")
                nc.gpsimd.tensor_tensor(sq[:, :, :], flat, flat, ALU.mult).then_inc(s_post, 1)

            def rms_norm(bb):
                pwait(s_newton, NEWTON * (bb + 1))
                pwait(s_post, 7 * bb + 3)
                nc.gpsimd.tensor_tensor(dn[:, :, :, :, :].rearrange("p i k r v -> p k i r v"), dif[:, :, :, :, :],
                                        rinv[:, :].rearrange("p (k i r) -> p k i r", k=KVH, i=NI).unsqueeze(4)
                                        .to_broadcast([P, KVH, NI, 2, 2 * HD]), ALU.mult).then_inc(s_post, 1)

            def layer_norm(bb):
                n = 7 * bb + 4
                pwait(s_bn, 8 * bb + 8)
                pwait(s_post, n)
                pwait(s_x1, 4 * bb)
                nc.gpsimd.tensor_scalar(vare[:, :], bag[:, :, 1], LN_EPS, None, ALU.add).then_inc(s_post, 1)
                pwait(s_post, n + 1)
                nc.gpsimd.tensor_tensor(rstd[:, :], vare[:, :], half[:, 0:NI], ALU.pow).then_inc(s_post, 1)
                pwait(s_post, n + 2)
                for i in range(NI):
                    m = nc.gpsimd.tensor_scalar(shift[:, i:i + 1], bag[:, i, 0:1], rstd[:, i:i + 1], -1.0, ALU.mult,
                                                ALU.mult)
                m.then_inc(s_post, 1)

            pool.wait_ge(s_half, 1)
            for a in range(2):
                add(0, a, 2 * a + 2)
                rest_of(0, a, 0)
                rest_of(0, a, 1)

            def body(b):
                for p in range(SUPER):
                    for u in range(NU):
                        if on(b, p, 2):
                            mask(b, p, u)
                        if u == 0 and on(b, p, 1):
                            negate(b, p)
                        if used(b, p, "q"):
                            if u == 18 and p < 2:
                                add(b + 1, p, uses_before(b, p, ("q_swap", "k_swap")[p]) + 1)
                            if u in (5, 9) and p in (1, 2):
                                rest_of(b + 1, p - 1, u // 9)
                        if p == 2 and u == 3 and (not isinstance(b, int) or b < B):
                            pwait(s_free, v_free(b))
                            if isinstance(b, int):
                                wait(pool, s_pv, NG * 4 * b)
                            else:
                                pwait(s_pv, NG * 4 * b)
                            if isinstance(b, int) and b == 0:
                                pool.wait_ge(s_vzero, 2)
                            nc.gpsimd.tensor_copy(v_aug[:, :, :, 0:2 * HD].rearrange("p i k v -> p (i k) v"),
                                                  v_new[:, :, :, :].rearrange("p i k v -> p (i k) v"))\
                                .then_inc(s_vaug, 1)
                        if used(b, p, "wo"):
                            if (p, u) == (2, 12):
                                over_total(b - 1)
                            if (p, u) == (2, 14):
                                difference(b - 1)
                            if (p, u) == (2, 16):
                                square(b - 1)
                            if (p, u) == (3, 0):
                                rms_norm(b - 1)
                            if (p, u) == (3, 10):
                                layer_norm(b - 1)

            def v_free(b):
                if isinstance(b, int) and b == 0:
                    return len(PREP)
                return uses_before(b - 1, 3, "v") + 1

            iterations(pool, body)

            def weights(j):
                nc.gpsimd.indirect_dma_start(out=wbuf[:, j % RING, :], out_offset=None, in_=w12,
                                             in_offset=bass.IndirectOffsetOnAxis(es_u[:, j:j + 1], 0))\
                    .then_inc(s_wg[j % RING], 16)

            pool.wait_ge(s_x1st, 16 * B)
            pool.wait_ge(s_pos, 1)
            for n in range(NTILE):
                nc.gpsimd.indirect_dma_start(out=x_sorted, out_offset=bass.IndirectOffsetOnAxis(pos_u[:, n:n + 1], 0),
                                             in_=x1_all[:, n, :], in_offset=None).then_inc(s_scat, 16)
                if 1 <= n <= RING:
                    if n == 1:
                        pool.wait_ge(s_pos, 2)
                    weights(n - 1)

            def scatter(j):
                pool.wait_ge(s_norm, 2 * (j + 1))
                for a in range(SLOT // P):
                    nc.gpsimd.indirect_dma_start(out=out,
                                                 out_offset=bass.IndirectOffsetOnAxis(row_u[:, j % RING, a:a + 1], 0),
                                                 in_=ynorm[:, j % 2, a, :], in_offset=None)\
                        .then_inc(s_outs[j % 2], 16)

            for j in range(NSLOT):
                par = j % 2
                pool.wait_ge(s_ln, LN_STEPS * (j + 1))
                wait(pool, s_norm, 2 * (j - 1))
                nc.gpsimd.tensor_tensor(rstd2[:, par], var2[:, par], half[:, 0:2], ALU.pow).then_inc(s_rs2, 1)
                pool.wait_ge(s_rs2, 3 * j + 1)
                for a in range(SLOT // P):
                    nc.gpsimd.tensor_scalar(shift2[:, par, a:a + 1], bag2[:, par, a, 0:1], rstd2[:, par, a:a + 1],
                                            -1.0, ALU.mult, ALU.mult).then_inc(s_rs2, 1)
                if j + RING < NSLOT:
                    weights(j + RING)
                if j:
                    scatter(j - 1)
            scatter(NSLOT - 1)

        @block.vector
        def _(dve):
            V = nc.vector
            V.memset(qa[:, :, :].rearrange("p k t -> p (k t)").bitcast(F32), 0.0).then_inc(s_clear, 1)
            V.memset(ka[:, 0:2].rearrange("p c k t -> p (c k t)").bitcast(F32), 0.0).then_inc(s_clear, 1)
            dve.wait_ge(s_const, ALL_CONST)
            V.tensor_tensor(lam_p[:, :, :], lam_s[:, 0:4:2, :], lam_s[:, 1:4:2, :], ALU.mult).then_inc(s_lam, 1)
            dve.wait_ge(s_lam, 1)
            V.tensor_reduce(lam_d[:, 0:2], lam_p[:, :, :], AX.X, ALU.add).then_inc(s_lam, 1)
            dve.wait_ge(s_lexp, 1)
            V.tensor_scalar(lam_n[:, :], lam_d[:, 3:4], lam_d[:, 2:3], -LAMBDA_INIT, ALU.subtract, ALU.add)\
                .then_inc(s_lam, 1)
            V.tensor_scalar(rms_c[:, :], rms_s[:, :], (1.0 - LAMBDA_INIT) * math.sqrt(2 * HD), None, ALU.mult)\
                .then_inc(s_lam, 1)
            dve.wait_ge(s_lam, 4)
            V.tensor_scalar(wo_n[:, :], wo_s[:, :], rms_c[:, 0:1], None, ALU.mult).then_inc(s_won, 1)

            def rotate(name, n, bn):
                k = PREP.index(name)
                wait(dve, s_split, 6 * bn + 3 * (k // 2) - 2)
                wait(dve, s_misc, n + 1)
                V.tensor_tensor((rot1, rot2)[k % 2][:, :], misc[:, :], rope[:, k, :], ALU.mult)\
                    .then_inc(s_free, 1)

            def inverse_root(bb):
                n = NEWTON * bb

                def step(k, ins):
                    ins.then_inc(s_newton, 1)
                    if k < NEWTON - 1:
                        wait(dve, s_newton, n + k + 1)

                wait(dve, s_ss, bb + 1)
                wait(dve, s_newton, n)
                step(0, V.tensor_scalar(nv[:, :], ss[:, :], 2 * HD * RMS_EPS, None, ALU.add))
                step(1, V.tensor_scalar(nint[:, :], nv[:, :].bitcast(I32), 1, None, ALU.logical_shift_right))
                step(2, V.tensor_scalar(rinv[:, :].bitcast(I32), nint[:, :], -1.0, float(0x5F3759DF), ALU.mult, ALU.add))
                k = 3
                for _ in range(3):
                    step(k, V.scalar_tensor_tensor(ny[:, :], rinv[:, :], -0.5, rinv[:, :], ALU.mult, ALU.mult))
                    step(k + 1, V.tensor_tensor(ny[:, :], ny[:, :], nv[:, :], ALU.mult))
                    step(k + 2, V.scalar_tensor_tensor(rinv[:, :], ny[:, :], 1.5, rinv[:, :], ALU.add, ALU.mult))
                    k += 3

            def row_max(b, p, u):
                kind, kk, c = UNITS[u]
                s = 4 * b + p
                bk = nat_b[u % 3]
                dst = mr[:, p % 2]
                if u == 0:
                    wait(dve, s_neg, 6 * (s - 2) + 2)
                wait(dve, s_nat, NU * s + u + 1)
                if kind == "A":
                    o, i = dst[:, 2 * c + kk, 6:7], bk[:, :]
                elif kind == "B":
                    o, i = dst[:, 2 * c + kk, 0:4], bk[:, :].rearrange("p (n t) -> p n t", t=P)
                else:
                    o, i = dst[:, 2 * c:2 * c + 2, 4], bk[:, :].rearrange("p (n t) -> p n t", n=2)
                V.tensor_reduce(o, i, AX.X, ALU.max).then_inc(s_max, 1)
                if u == NU - 1:
                    wait(dve, s_max, (NU + 1) * s + NU)
                    V.tensor_reduce(dst[:, :, 5:6], dst[:, :, 1:4], AX.X, ALU.max).then_inc(s_max, 1)

            def take(b, p, u):
                for name in misc_at(b, p, u):
                    if name not in ("q", "q_swap", "k", "k_swap", "wo", "router"):
                        continue
                    n = uses_before(b, p, name)
                    if name == "wo":
                        bb = b - 1
                        wait(dve, s_xn, 16 * (bb + 1))
                        wait(dve, s_x1, 4 * bb)
                        wait(dve, s_misc, n + 1)
                        V.tensor_tensor(res[:, :, :], misc[:, :].rearrange("p (i d) -> p i d", i=NI), xn[:, :, :],
                                        ALU.add).then_inc(s_free, 1)
                        wait(dve, s_free, n + 1)
                        for i in range(NI):
                            V.bn_stats(bst[:, i, :], res[:, i, :]).then_inc(s_bn, 1)
                        wait(dve, s_bn, 8 * bb + 4)
                        dve.nop(nofuse=True)
                        for i in range(NI):
                            V.bn_aggr(bag[:, i, :], bst[:, i, :]).then_inc(s_bn, 1)
                    elif name == "router":
                        wait(dve, s_misc, n + 1)
                        V.tensor_tensor(logit[:, bass.ds((b - 1) * NI, NI), :],
                                        misc[:, 0:NI * NX].rearrange("p (i e) -> p i e", i=NI),
                                        rb_s[:, :].unsqueeze(1).to_broadcast([P, NI, NX]), ALU.add)\
                            .then_inc(s_free, 1)
                    else:
                        rotate(name, n, b + 1)

            for n, name in enumerate(PREP[:4]):
                rotate(name, n, 0)

            def body(b):
                for p in range(SUPER):
                    for u in range(NU):
                        if on(b, p, 0):
                            row_max(b, p, u)
                        if u:
                            take(b, p, u - 1)
                        if used(b, p, "wo"):
                            bb = b - 1
                            if (p, u) == (2, 12):
                                wait(dve, s_free, uses_before(b, 2, "sel1") + 1)
                                V.reciprocal(rl[:, :, :, :], on_s[:, :, :, :, 2 * HD]).then_inc(s_rl, 1)
                                wait(dve, s_rl, 2 * bb + 1)
                                second = rl[:, :, :, :].rearrange("p k i (r j) -> p (k i r) j", j=2)[:, :, 1]
                                V.tensor_scalar(second, second, lam_n[:, 0:1], None, ALU.mult).then_inc(s_rl, 1)
                            if (p, u) == (2, 18):
                                wait(dve, s_post, 7 * bb + 3)
                                V.tensor_reduce(ss[:, :], sq[:, :, :], AX.X, ALU.add).then_inc(s_ss, 1)
                            if (p, u) == (3, 0):
                                inverse_root(bb)

            iterations(dve, body)

            E_, D_ = rt, [P, NTILE, NX]
            count = [0]

            def step(ins):
                count[0] += 1
                ins.then_inc(s_route, 1)
                dve.wait_ge(s_route, count[0])

            io_k, io_j = iota[:, 0:16], iota[:, 16:16 + NSLOT]
            io_e, io_p = iota[:, 16 + NSLOT:16 + NSLOT + NX], iota[:, 16 + NSLOT + NX:17 + NSLOT + NX]
            io_t = iota[:, 17 + NSLOT + NX:]

            def over(a, shape, axis):
                return a.unsqueeze(axis).to_broadcast(shape)

            dve.wait_ge(s_free, TOTAL_MISC)
            step(V.tensor_reduce(rmax[:, :], logit[:, :, :], AX.X, ALU.max))
            step(V.tensor_tensor(E_["d"][:, :, :], logit[:, :, :], over(rmax[:, :], D_, 2), ALU.subtract))
            step(V.tensor_tensor(E_["t"][:, :, :], logit[:, :, :], over(rmax[:, :], D_, 2), ALU.is_equal))
            step(V.scalar_tensor_tensor(E_["a"][:, :, :], E_["t"][:, :, :], -float(NX), over(io_e, D_, 1),
                                        ALU.mult, ALU.add))
            step(V.tensor_reduce(rmin[:, :], E_["a"][:, :, :], AX.X, ALU.min))
            dve.wait_ge(s_rexp, 1)
            step(V.tensor_reduce(rsum[:, :], E_["e"][:, :, :], AX.X, ALU.add))
            step(V.reciprocal(x1_all[:, :, E], rsum[:, :]))
            step(V.tensor_copy(x1_all[:, :, E + 1], io_t))
            step(V.tensor_copy(E_["z"][:, :, :], E_["a"][:, :, :]))
            step(V.tensor_tensor(E_["oh"][:, :, :], E_["a"][:, :, :], over(rmin[:, :], D_, 2), ALU.is_equal))
            dve.wait_ge(s_rank, 1)
            step(V.tensor_copy(E_["b"][:, :, :], banks[1][:, 0:NTILE * NX].rearrange("p (n e) -> p n e", e=NX)))
            step(V.tensor_copy(E_["a"][:, :, :], E_["b"][:, :, :]))
            cur, nxt, d = "b", "c", 1
            while d < NTILE:
                step(V.tensor_copy(E_[nxt][:, 0:d, :], E_[cur][:, 0:d, :]))
                step(V.tensor_tensor(E_[nxt][:, d:, :], E_[cur][:, d:, :], E_[cur][:, 0:NTILE - d, :], ALU.add))
                cur, nxt, d = nxt, cur, 2 * d
            total = E_[cur][:, NTILE - 1, :]
            cs = [P, NX, 16]
            step(V.tensor_tensor(cmp_n[:, :, :], over(total, cs, 2), over(io_k, cs, 1), ALU.is_gt))
            step(V.tensor_reduce(nsl[:, 0, :], cmp_n[:, :, :], AX.X, ALU.add))
            a = 0
            for d in (1, 2, 4):
                step(V.tensor_copy(nsl[:, a + 1, 0:d], nsl[:, a, 0:d]))
                step(V.tensor_tensor(nsl[:, a + 1, d:], nsl[:, a, d:], nsl[:, a, 0:NX - d], ALU.add))
                a += 1
            step(V.tensor_tensor(nsl[:, 4, :], nsl[:, 3, :], nsl[:, 0, :], ALU.subtract))
            step(V.tensor_scalar(nsl[:, 4, :], nsl[:, 4, :], float(SLOT), None, ALU.mult))
            step(V.tensor_tensor(E_[nxt][:, :, :], E_[cur][:, :, :], E_["a"][:, :, :], ALU.subtract))
            step(V.tensor_tensor(E_["t"][:, :, :], E_[nxt][:, :, :],
                                 banks[0][:, 0:NTILE * NX].rearrange("p (n e) -> p n e", e=NX), ALU.add))
            step(V.tensor_tensor(E_["d"][:, :, :], E_["t"][:, :, :], over(nsl[:, 4, :], D_, 1), ALU.add))
            step(V.tensor_tensor(E_["t"][:, :, :], E_["d"][:, :, :], E_["oh"][:, :, :], ALU.mult))
            step(V.tensor_reduce(pos_f[:, :], E_["t"][:, :, :], AX.X, ALU.add))
            V.tensor_copy(pos_u[:, :], pos_f[:, :]).then_inc(s_pos, 1)
            ss_ = [P, NSLOT, NX - 1]
            step(V.tensor_tensor(cmp_s[:, :, :], over(nsl[:, 3, 0:NX - 1], ss_, 1), over(io_j, ss_, 2), ALU.is_le))
            step(V.tensor_reduce(es[:, :], cmp_s[:, :, :], AX.X, ALU.add))
            step(V.tensor_scalar(es_r[:, :], es[:, :], float(P), io_p, ALU.mult, ALU.add))
            V.tensor_copy(es_u[:, :], es_r[:, :]).then_inc(s_pos, 1)

            def take_x(j, n):
                wait(dve, s_xturn, j + 1)
                wait(dve, s_h, NF * (j - 1))
                V.tensor_copy(xst[:, n % 2, :], banks[4][:, 0:SLOT]).then_inc(s_xst, 1)

            def mix(j, k, n):
                par, m = n % 2, LN_STEPS * j
                wait(dve, s_y, j + 1)
                wait(dve, s_outs[par], 32 * (2 * k + n // 2 - 1))
                wait(dve, s_norm, 2 * (j - 1))
                wait(dve, s_ln, m)
                V.tensor_copy(row_u[:, n, :], xs[:, n, :, E + 1]).then_inc(s_ln, 1)
                for a in range(SLOT // P):
                    V.scalar_tensor_tensor(ymix[:, par, a, :], banks[5 + par][:, a * P:(a + 1) * P],
                                           xs[:, n, a, E:E + 1], xs[:, n, a, 0:E], ALU.mult, ALU.add)\
                        .then_inc(s_ln, 1)
                wait(dve, s_ln, m + 3)
                for a in range(SLOT // P):
                    V.bn_stats(bst2[:, a, :], ymix[:, par, a, :]).then_inc(s_ln, 1)
                wait(dve, s_ln, m + 5)
                dve.nop(nofuse=True)
                for a in range(SLOT // P):
                    V.bn_aggr(bag2[:, par, a, :], bst2[:, a, :]).then_inc(s_ln, 1)
                wait(dve, s_ln, m + 7)
                V.tensor_scalar(var2[:, par], bag2[:, par, :, 1], LN_EPS, None, ALU.add).then_inc(s_ln, 1)

            def slot(j, k, n):
                for f in range(NF):
                    if f == NF - 1 and (not isinstance(j, int) or j + 1 < NSLOT):
                        take_x(j + 1, (n + 1) % RING)
                    wait(dve, s_silu, NF * j + f + 1)
                    if f == 0:
                        wait(dve, s_y, j - 1)
                    V.tensor_tensor(u_s[:, n % 2, f, :], sa[:, f, :], banks[f][:, SLOT:2 * SLOT], ALU.mult)\
                        .then_inc(s_u, 1)
                if not isinstance(j, int) or j >= 1:
                    mix(j - 1, k - (n == 0), (n - 1) % RING)

            take_x(0, 0)
            slots(dve, slot)
            mix(NSLOT - 1, (NSLOT - 1) // RING, (NSLOT - 1) % RING)


def kernel(L0_attn_x, L0_attn_Wq, L0_attn_Wk, L0_attn_Wv, L0_attn_Wo, L0_attn_lambda_q1, L0_attn_lambda_k1,
           L0_attn_lambda_q2, L0_attn_lambda_k2, L0_attn_rms_w, L0_ffn_router_w, L0_ffn_router_b, L0_ffn_w1,
           L0_ffn_w2):
    import ml_dtypes
    import concourse.bacc as bacc
    from concourse.bass_utils import run_bass_kernel_spmd

    f = np.float32
    x = np.ascontiguousarray(L0_attn_x).reshape(B * T, E)
    r, j, d, kv = np.meshgrid(range(2), range(2), range(HD), range(KVH), indexing="ij")
    q_col = (((2 * kv + r) * 2 + j) * HD + d).ravel()
    q_swap = (((2 * kv + r) * 2 + j) * HD + (d ^ 2)).ravel()
    k_col = ((kv * 2 + j) * HD + d).ravel()
    k_swap = ((kv * 2 + j) * HD + (d ^ 2)).ravel()
    Wq, Wk, w2 = np.asarray(L0_attn_Wq), np.asarray(L0_attn_Wk), np.asarray(L0_ffn_w2)
    inv_freq = 1.0 / 10000.0 ** (np.arange(0, HD, 2, dtype=f) / HD)
    freqs = np.outer(np.arange(T, dtype=f), inv_freq)
    dd = d.ravel()
    cos = np.cos(freqs).astype(f).T[dd % 2]
    sin = np.sin(freqs).astype(f).T[dd % 2] * np.where(dd < 2, 1, -1)[:, None]
    scale = HD ** -0.5
    rope = np.stack([cos * scale, sin * scale, cos, sin], 1).astype(f)
    pick = np.zeros((P, 4 * VW), f)
    for c in range(4):
        for v in range(VW):
            pick[32 * c + v, c * VW + v] = 1
    before = (np.arange(P)[:, None] < np.arange(P)[None, :]).astype(f)
    iota = np.concatenate([np.arange(16) * SLOT, np.arange(NSLOT), np.arange(NX)]).astype(f)
    rows = np.arange(B * T, dtype=f).reshape(NTILE, P).T
    iota = np.concatenate([np.broadcast_to(iota, (P, iota.size)), np.arange(P, dtype=f)[:, None], rows], 1)
    pad = np.zeros((NSLOT * SLOT, XW), f)
    pad[:, E + 1] = B * T + np.arange(NSLOT * SLOT)
    causal = np.where(np.arange(P)[None, :] > np.arange(P)[:, None], MASKED, 0.0)
    arrays = {
        "xT": x.T, "x": x, "wq": Wq[:, q_col], "wqs": Wq[:, q_swap], "wk": Wk[:, k_col], "wks": Wk[:, k_swap],
        "wv": np.asarray(L0_attn_Wv), "wo": np.asarray(L0_attn_Wo),
        "lam": np.concatenate([np.asarray(a) for a in (L0_attn_lambda_q1, L0_attn_lambda_k1, L0_attn_lambda_q2,
                                                       L0_attn_lambda_k2)]),
        "rms": np.tile(np.asarray(L0_attn_rms_w), H)[:, None],
        "router_w": np.asarray(L0_ffn_router_w), "router_b": np.asarray(L0_ffn_router_b),
        "w12": np.concatenate([np.asarray(L0_ffn_w1), w2.reshape(NX, NF, P, E).transpose(0, 2, 1, 3)
                               .reshape(NX, P, NF * E)], 2).reshape(NX * P, 3 * FFN),
        "c_rope": rope, "c_ident": np.eye(P, dtype=f),
        "c_mask": np.concatenate([np.eye(P), causal], 1).astype(ml_dtypes.bfloat16),
        "c_sel": pick, "c_tri": np.stack([before, np.ones((P, P), f)], 1), "c_iota": iota,
        "c_one": np.repeat([1, 0], MROWS)[:, None].repeat(KVH * T, 1).astype(ml_dtypes.bfloat16),
        "c_pad": pad,
    }
    arrays = {"in_" + k: np.ascontiguousarray(v) for k, v in arrays.items()}
    nc = bacc.Bacc("TRN2", target_bir_lowering=False, num_devices=1)
    args = [nc.dram_tensor(k, v.shape, mybir.dt.from_np(v.dtype), kind="ExternalInput").ap()
            for k, v in arrays.items()]
    args.append(nc.dram_tensor("out_dram", (B * T + NSLOT * SLOT, E), F32, kind="ExternalOutput").ap())
    build(nc, *args)
    got = run_bass_kernel_spmd(nc, [arrays], core_ids=[0])
    return got.results[0]["out_dram"][0:B * T].reshape(B, T, E)
```
